# Optimizing a Trainium2 kernel written in Bass

```python
import numpy as np
import jax
import jax.numpy as jnp

def _softmax(x, axis=-1):
    return jax.nn.softmax(x, axis=axis)

def _gelu(x):
    return jax.nn.gelu(x, approximate=True)

def _silu(x):
    return jax.nn.silu(x)

def _sigmoid(x):
    return jax.nn.sigmoid(x)

def _layernorm(x, axis=-1, eps=1e-05):
    m = jnp.mean(x, axis=axis, keepdims=True)
    v = jnp.var(x, axis=axis, keepdims=True)
    return (x - m) / jnp.sqrt(v + eps)

def _scatter_add(tgt, idx, src, axis=0):
    return tgt.at[idx].add(src)

def _segment_sum(src, seg, n):
    return jax.ops.segment_sum(src, seg, n)
kernel_name = 'mk_gnn_resnorm_d2_gnn_r8_e57a64'

def setup_inputs(seed: int=0):
    np.random.seed(seed)
    _w = jnp.asarray

    def _rec_inputs():
        import jax
        import jax.numpy as jnp
        _gk = jax.random.key(seed)
        x = -0.0005121 + 1.001 * jax.random.normal(jax.random.fold_in(_gk, 1), (12500, 64), jnp.float32)
        src = jax.random.randint(jax.random.fold_in(_gk, 2), (400000,), 0, 12500, jnp.int32)
        dst = jax.random.randint(jax.random.fold_in(_gk, 3), (400000,), 0, 12500, jnp.int32)
        _o = jnp.argsort(dst, stable=True)
        src = src[_o]
        dst = dst[_o]
        return (x, src, dst)
    x, src, dst = _rec_inputs()

    def _L0_gnn_setup():
        import jax, jax.numpy as jnp
        import numpy as np
        N_NODES = 6250
        NEG_SLOPE = 0.01
        key = jax.random.key(seed)
        ks = jax.random.split(key, 5)
        N, E, D = (N_NODES, 100000, 64)
        x = jax.random.normal(ks[0], (N, D), dtype=jnp.float32)
        edge_index = jax.random.randint(ks[1], (2, E), 0, N, dtype=jnp.int64)
        W1 = jax.random.normal(ks[2], (2 * D, D), dtype=jnp.float32) * (1.0 / np.sqrt(2 * D))
        b1 = jnp.zeros((D,), dtype=jnp.float32)
        W2 = jax.random.normal(ks[3], (D, D), dtype=jnp.float32) * (1.0 / np.sqrt(D))
        b2 = jnp.zeros((D,), dtype=jnp.float32)
        return {'x': x, 'edge_index': edge_index, 'W1': W1, 'b1': b1, 'W2': W2, 'b2': b2}
    _L0_gnn_all = _L0_gnn_setup()
    _L0_gnn_in = {k: v for k, v in _L0_gnn_all.items() if k in ('W1', 'b1', 'W2', 'b2')}
    del _L0_gnn_all

    def _L1_gnn_setup():
        import jax, jax.numpy as jnp
        import numpy as np
        DIM = 64
        HEADS = 4
        N_NODES = 6250
        N_EDGES = 100000
        NEG_SLOPE = 0.2
        key = jax.random.key(seed)
        k1, k2, k3, k4, k5 = jax.random.split(key, 5)
        meta_x = jax.random.normal(k1, (N_NODES, DIM), dtype=jnp.float32)
        meta_edge_index = jax.random.randint(k2, (2, N_EDGES), 0, N_NODES, dtype=jnp.int64)
        glorot = float(np.sqrt(2.0 / (DIM + HEADS * DIM)))
        W = jax.random.normal(k3, (DIM, HEADS * DIM), dtype=jnp.float32) * glorot
        att_src = jax.random.normal(k4, (1, HEADS, DIM), dtype=jnp.float32) * glorot
        att_dst = jax.random.normal(k5, (1, HEADS, DIM), dtype=jnp.float32) * glorot
        bias = jnp.zeros((DIM,), dtype=jnp.float32)
        return {'meta_x': meta_x, 'meta_edge_index': meta_edge_index, 'W': W, 'att_src': att_src, 'att_dst': att_dst, 'bias': bias}
    _L1_gnn_all = _L1_gnn_setup()
    _L1_gnn_in = {k: v for k, v in _L1_gnn_all.items() if k in ('W', 'att_src', 'att_dst', 'bias')}
    del _L1_gnn_all
    return {'x': x, 'src': src, 'dst': dst, 'L0_gnn_W1': _L0_gnn_in['W1'], 'L0_gnn_b1': _L0_gnn_in['b1'], 'L0_gnn_W2': _L0_gnn_in['W2'], 'L0_gnn_b2': _L0_gnn_in['b2'], 'L1_gnn_W': _L1_gnn_in['W'], 'L1_gnn_att_src': _L1_gnn_in['att_src'], 'L1_gnn_att_dst': _L1_gnn_in['att_dst'], 'L1_gnn_bias': _L1_gnn_in['bias']}

def reference(x, src, dst, L0_gnn_W1, L0_gnn_b1, L0_gnn_W2, L0_gnn_b2, L1_gnn_W, L1_gnn_att_src, L1_gnn_att_dst, L1_gnn_bias):
    import jax
    import jax.numpy as jnp

    def _L0_gnn_ref(x, edge_index, W1, b1, W2, b2):
        import jax, jax.numpy as jnp
        import numpy as np
        N_NODES = 6250
        NEG_SLOPE = 0.01
        src = edge_index[0]
        dst = edge_index[1]
        x_i = x[dst]
        x_j = x[src]
        msg_in = jnp.concatenate([x_i, x_j - x_i], axis=-1)
        h = jax.nn.leaky_relu(msg_in @ W1 + b1, NEG_SLOPE)
        h = jax.nn.leaky_relu(h @ W2 + b2, NEG_SLOPE)
        out = jax.ops.segment_sum(h, dst, num_segments=x.shape[0])
        return out

    def _L1_gnn_ref(meta_x, meta_edge_index, W, att_src, att_dst, bias):
        import jax, jax.numpy as jnp
        import numpy as np
        DIM = 64
        HEADS = 4
        N_NODES = 6250
        N_EDGES = 100000
        NEG_SLOPE = 0.2
        N = meta_x.shape[0]
        loops = jnp.arange(N, dtype=meta_edge_index.dtype)
        edge = jnp.concatenate([meta_edge_index, jnp.stack([loops, loops])], axis=1)
        src, dst = (edge[0], edge[1])
        x = (meta_x @ W).reshape(N, HEADS, DIM)
        a_src = jnp.sum(x * att_src, axis=-1)
        a_dst = jnp.sum(x * att_dst, axis=-1)
        logits = a_src[src] + a_dst[dst]
        logits = jax.nn.leaky_relu(logits, NEG_SLOPE)
        seg_max = jax.ops.segment_max(logits, dst, num_segments=N)
        ex = jnp.exp(logits - seg_max[dst])
        seg_sum = jax.ops.segment_sum(ex, dst, num_segments=N)
        alpha = ex / (seg_sum[dst] + 1e-16)
        msg = x[src] * alpha[:, :, None]
        out = jax.ops.segment_sum(msg, dst, num_segments=N)
        return out.mean(axis=1) + bias
    edge_index = jnp.stack([src, dst])
    x = _layernorm(x + _L0_gnn_ref(x, edge_index, L0_gnn_W1, L0_gnn_b1, L0_gnn_W2, L0_gnn_b2), axis=-1)
    x = _layernorm(x + _L1_gnn_ref(x, edge_index, L1_gnn_W, L1_gnn_att_src, L1_gnn_att_dst, L1_gnn_bias), axis=-1)
    return x

_drawn_inputs = setup_inputs


def setup_inputs(seed=0):
    import zlib

    import numpy as np

    out = dict(_drawn_inputs(seed))
    spreads = {'L0_gnn_b1': (0.0, 0.1), 'L0_gnn_b2': (0.0, 0.1), 'L1_gnn_bias': (0.0, 0.1)}
    factors = {'L1_gnn_att_src': 4.224, 'L1_gnn_att_dst': 8.0}
    for name, (base, spread) in spreads.items():
        noise = np.random.default_rng([zlib.crc32(name.encode()), seed]).standard_normal(out[name].shape)
        drawn = base * np.exp(spread * noise) if base else spread * noise
        out[name] = jnp.asarray(drawn.astype(out[name].dtype))
    for name, factor in factors.items():
        out[name] = (out[name] * factor).astype(out[name].dtype)
    return out
```

```python
import concourse.bass as bass
from concourse import mybir
from contextlib import ExitStack

N, E, D, H = 12500, 400000, 64, 4
P = 128
NB = -(-N // P)
LAST = N - (NB - 1) * P
TG = 8
GE = TG * P
GS = 8
TS = TG * GS
NT = E // P
NG = -(-E // GE)
NS = -(-NG // GS)
G = NS * GS
T = G * TG
EP = T * P
XW = D + H
UW = H * (D + 1)
YW = UW + H + 1
BIG = 1.0e30
PADNODE = 1000000
NC = -(-NT // P)
RL = NT - (NC - 1) * P
NU = -(-NC // 4)
NCH = 7
BC = NB // NCH
LN_OPS = 8
EPS = 1e-5


def build(nc, x, src, dst, W1, b1, W2, b2, W, att_src, att_dst, bias, out, q_dram, x_dram, srcT_dram,
          dstT_dram, dst_dram):
    f32, i32 = mybir.dt.float32, mybir.dt.int32
    ALU, ACT, AX = mybir.AluOpType, mybir.ActivationFunctionType, mybir.AxisListType
    ds = bass.ds
    ctx = ExitStack()
    with ctx:
        def sb(name, shape, dt=f32):
            return ctx.enter_context(nc.sbuf_tensor(name, shape, dt))

        def sem(name):
            return ctx.enter_context(nc.semaphore(name))

        state = sb("state", [P, NB * UW])
        x1 = sb("x1", [P, NB, XW])
        gbuf = sb("gbuf", [P, 2 * TS * XW])
        S = sb("S", [P, TG, P])
        ST = sb("ST", [P, TG, P])
        Y = sb("Y", [P, TG, YW])
        rowD = sb("rowD", [32, GE], i32)
        rowR = sb("rowR", [32, GE + 1])
        rowA = sb("rowA", [P, GE])
        rowF = rowA[0:32, :]
        idx = sb("idx", [P, 2, TS], i32)
        dstc = sb("dstc", [P, 2, TS])
        edgeM = sb("edgeM", [P, TS, H])
        edgeE = sb("edgeE", [P, TS, H + 1])
        edgeA = sb("edgeA", [P, TG, 32])
        ident = sb("ident", [P, P])
        iota = sb("iota", [P, P])
        blk = sb("blk", [P, NB])
        Bt = sb("Bt", [1, G + 1], i32)
        rel = sb("rel", [P, TG])
        adst = sb("adst", [P, NB, H])
        Mx = sb("Mx", [P, NB, H])
        zz = sb("zz", [P, 2, TG, H])
        lz = sb("lz", [P, 2, TG, H])
        dw = sb("dw", [P, TG, H])
        nz = sb("nz", [P, 3, H])
        pen = sb("pen", [P, 1])
        mnew = sb("mnew", [P, H])
        dd = sb("dd", [P, 2, H])
        ee = sb("ee", [P, 2, H])
        w1 = sb("w1", [D + 1, 2 * D])
        w2 = sb("w2", [D + 1, D])
        wsb = sb("wsb", [D, H * D])
        attb = sb("attb", [D, 2, H * D])
        va = sb("va", [D, 2 * H])
        wf = sb("wf", [P, 2, D])
        biasr = sb("biasr", [1, D])
        ones = sb("ones", [1, P])
        st2 = sb("st2", [P, 2, D + 1])
        stT = sb("stT", [D + 1, 2, P])
        mean = sb("mean", [P, NB])
        var = sb("var", [P, NB])
        dum = sb("dum", [P, 1])

        ps = [ctx.enter_context(nc.psum_tensor(f"ps{i}", [P, 512], f32)) for i in range(8)]

        x0 = state[:, 0:NB * D].rearrange("p (b d) -> p b d", d=D)
        pt = state[:, NB * D:2 * NB * D].rearrange("p (b d) -> p b d", d=D)
        acc0 = state[:, 2 * NB * D:3 * NB * D].rearrange("p (b d) -> p b d", d=D)
        qst = state[:, 3 * NB * D:4 * NB * D].rearrange("p (b d) -> p b d", d=D)
        acc = state[:, :].rearrange("p (b h d) -> p b h d", h=H, d=D + 1)
        g0 = gbuf[:, 0:2 * TS * D].rearrange("p (t d) -> p t d", d=D)
        g1 = gbuf[:, :].rearrange("p (t d) -> p t d", d=XW)
        h1 = Y[:, :, 0:D + 1]
        h2 = Y[:, :, 80:80 + D]
        az1 = Y[:, :, 150:150 + D]
        az2 = Y[:, :, 150:150 + D]
        h1T = rowA[0:D + 1, :].rearrange("p (t e) -> p t e", e=P)
        rows_i = x1[:, :, :].rearrange("p b d -> p (b d)")[:, 0:3200].bitcast(i32)
        rows_f = x1[:, :, :].rearrange("p b d -> p (b d)")[:, 3200:6400]
        srcT = gbuf[:, 0:T].bitcast(i32)
        dstT = gbuf[:, T:2 * T]
        ln_t = gbuf[:, 0:BC * D].rearrange("p (b d) -> p b d", d=D)

        names = "load clr pad cst idn b_ld bt rows_in rf rt rc q_out t_out d_out".split()
        s = {n: sem("s_" + n) for n in names}
        idx_in = [sem("idx_in0"), sem("idx_in1")]
        dst_in = [sem("dst_in0"), sem("dst_in1")]
        gath = [[sem(f"gath{l}{p}") for p in range(2)] for l in range(2)]
        row_in = sem("row_in")
        free_g = sem("free_g")
        free_d = sem("free_d")
        L = [{n: sem(f"l{l}_{n}") for n in
              "rel S stp sts z az h htp hts z2 az2 h2 U acc ad w e dv".split()} for l in range(2)]
        sgp, sgv = sem("sg_pe"), sem("sg_dve")
        lnv = sem("ln_dve")
        lna = sem("ln_act")
        vch = sem("dve_chain")
        tab0, tab1, fin = [{n: sem(f"{t}_{n}") for n in "st tp tc m v".split()}
                           for t in ("tab0", "tab1", "fin")]
        idle = sem("idle")
        x_out = sem("x_out")
        o_out = sem("o_out")

        block = ctx.enter_context(nc.Block())

        def supers(eng, body):
            with eng.Fori(0, NS // 2) as q:
                body(q * 2, q, 0)
                body(q * 2 + 1, q, 1)
            if NS % 2:
                body(NS - 1, NS // 2, 0)

        def apart(eng):
            eng.sem_inc(idle, 1)

        def steps(eng, i, step):
            apart(eng)
            with eng.Fori(0, GS) as r:
                g = i * GS + r
                b0 = eng.value_load(Bt[0:1, ds(g, 1)], min_val=0, max_val=NB - 1)
                b1 = eng.value_load(Bt[0:1, ds(g + 1, 1)], min_val=0, max_val=NB - 1)
                with eng.Fori(b0, b1 + 1) as b:
                    step(g + b, r, b)

        @block.sync
        def _(sp):
            xr = x[0:(NB - 1) * P, :].rearrange("(b p) d -> p b d", p=P)
            sp.wait_ge(s["clr"], 1)
            sp.dma_start(x0[:, 0:NB - 1, :], xr).then_inc(s["load"], 16)
            sp.dma_start(x0[0:LAST, NB - 1, :], x[(NB - 1) * P:N, :]).then_inc(s["load"], 16)
            sp.dma_start(w1[0:D, 0:D], W1[0:D, :]).then_inc(s["load"], 16)
            sp.dma_start(w1[0:D, D:2 * D], W1[D:2 * D, :]).then_inc(s["load"], 16)
            sp.dma_start(w1[D:D + 1, 0:D], b1.rearrange("(a d) -> a d", a=1)).then_inc(s["load"], 16)
            sp.dma_start(w2[0:D, :], W2[:, :]).then_inc(s["load"], 16)
            sp.dma_start(w2[D:D + 1, :], b2.rearrange("(a d) -> a d", a=1)).then_inc(s["load"], 16)
            sp.dma_start(wsb[:, :], W[:, :]).then_inc(s["load"], 16)
            sp.dma_start(attb[:, 0, :], att_src.rearrange("a h d -> a (h d)").to_broadcast([D, H * D])
                         ).then_inc(s["load"], 16)
            sp.dma_start(attb[:, 1, :], att_dst.rearrange("a h d -> a (h d)").to_broadcast([D, H * D])
                         ).then_inc(s["load"], 16)
            for h in range(H):
                sp.dma_start(wf[(h % 2) * D:(h % 2 + 1) * D, h // 2, :], W[:, h * D:(h + 1) * D]
                             ).then_inc(s["load"], 16)
            sp.dma_start(biasr[:, :], bias.rearrange("(a d) -> a d", a=1)).then_inc(s["load"], 16)
            sp.dma_start(dst_dram[0:E].rearrange("(a c) -> a c", a=16),
                         dst.rearrange("(a c) -> a c", a=16)).then_inc(s["d_out"], 16)
            sp.wait_ge(s["pad"], 1)
            sp.dma_start(dst_dram[E:EP].rearrange("(a c) -> a c", a=2),
                         rowD[0:2, 0:(EP - E) // 2]).then_inc(s["d_out"], 16)
            sp.wait_ge(s["rc"], NU)
            sp.dma_start(srcT_dram[:, :], srcT).then_inc(s["t_out"], 16)
            sp.wait_ge(s["rc"], 2 * NU)
            sp.dma_start(dstT_dram[:, :], dstT).then_inc(s["t_out"], 16)
            sp.wait_ge(tab0["v"], NB // 2)
            sp.dma_start(q_dram.rearrange("(b p) d -> p b d", p=P), qst).then_inc(s["q_out"], 16)
            sp.wait_ge(s["t_out"], 32)

            for l in range(2):
                def chunk(i, q, half):
                    sp.wait_ge(gath[l][half], q * (16 * TS))
                    sp.dma_start(idx[:, half, :], srcT_dram[:, ds(i * TS, TS)]).then_inc(idx_in[half], 16)
                    sp.wait_ge(free_d, i + l * NS)
                    sp.dma_start(dstc[:, half, :], dstT_dram[:, ds(i * TS, TS)]).then_inc(dst_in[half], 16)
                    if l:
                        sp.wait_ge(sgv, i * 4)
                        for h in range(H):
                            sp.dma_start(rowD[h * GS:(h + 1) * GS, :],
                                         dst_dram[ds(i * (GS * GE), GS * GE)].rearrange("(g e) -> g e", g=GS)
                                         ).then_inc(row_in, 16)
                if l:
                    sp.wait_ge(s["d_out"], 32)
                    sp.wait_ge(gath[0][0], 16 * TS * (NS - NS // 2))
                    sp.wait_ge(gath[0][1], 16 * TS * (NS // 2))
                supers(sp, chunk)
                if l == 0:
                    sp.wait_ge(tab1["v"], 2 * (NB // 2))
                    sp.dma_start(x_dram.rearrange("(b p) d -> p b d", p=P), x1[:, :, :]).then_inc(x_out, 16)
            sp.wait_ge(lnv, 2 * NCH * LN_OPS)
            sp.dma_start(out[0:(NB - 1) * P, :].rearrange("(b p) d -> p b d", p=P),
                         x1[:, 0:NB - 1, 0:D]).then_inc(o_out, 16)
            sp.dma_start(out[(NB - 1) * P:N, :], x1[0:LAST, NB - 1, 0:D]).then_inc(o_out, 16)
            sp.wait_ge(o_out, 32)

        @block.gpsimd
        def _(pool):
            nc.gpsimd.iota(iota[:, :], [[1, P]], base=0, channel_multiplier=0,
                           allow_small_or_imprecise_dtypes=True).then_inc(s["cst"], 1)
            nc.gpsimd.iota(blk[:, :], [[P, NB]], base=0, channel_multiplier=0,
                           allow_small_or_imprecise_dtypes=True).then_inc(s["cst"], 1)
            nc.gpsimd.memset(ident[:, :], 0.0).then_inc(s["idn"], 1)
            pool.wait_ge(s["idn"], 1)
            nc.gpsimd.affine_select(out=ident[:, :], in_=ident[:, :], compare_op=ALU.not_equal, fill=1.0,
                                    base=0, pattern=[[-1, P]], channel_multiplier=1).then_inc(s["idn"], 1)
            for l in range(2):
                if l == 0:
                    pool.wait_ge(s["q_out"], 16)
                    pool.wait_ge(s["t_out"], 32)
                else:
                    pool.wait_ge(x_out, 16)

                def gathers(i, q, half):
                    n = q + 1 + (0 if l == 0 else (NS - NS // 2 if half == 0 else NS // 2))
                    pool.wait_ge(idx_in[half], n * 16)
                    pool.wait_ge(free_g, i + l * NS)
                    apart(pool)
                    for t in range(TS):
                        o = (g1 if l else g0)[:, half * TS + t, :]
                        nc.gpsimd.indirect_dma_start(
                            o, None, x_dram if l else q_dram,
                            bass.IndirectOffsetOnAxis(ap=idx[:, half, t:t + 1], axis=0)
                        ).then_inc(gath[l][half], 16)
                supers(pool, gathers)

        @block.vector
        def _(dve):
            v = nc.vector
            count = [0]

            def link(ins):
                count[0] += 1
                ins.then_inc(vch, 1)
                dve.wait_ge(vch, count[0])

            link(v.memset(x0[:, NB - 1, :], 0.0))
            link(v.memset(ones[:, :], 1.0))
            v.memset(w1[D:D + 1, D:2 * D], 0.0).then_inc(s["clr"], 1)
            v.memset(rowD[:, :], PADNODE).then_inc(s["pad"], 1)
            link(v.memset(st2[:, :, D:D + 1], 1.0))
            link(v.memset(acc0, 0.0))
            link(v.memset(rowR[:, 0:1], -BIG))
            link(v.memset(rowR[:, GE:GE + 1], -BIG))
            link(v.memset(srcT[:, NT:T], 0))
            link(v.memset(dstT[:, NT:T], float(PADNODE)))
            dve.wait_ge(s["b_ld"], 16)
            link(v.tensor_scalar(Bt[0:1, 0:NG], Bt[0:1, 0:NG], 7, None, ALU.arith_shift_right))
            v.memset(Bt[0:1, NG:G + 1], NB - 1).then_inc(s["bt"], 1)
            for k in range(2):
                dve.wait_ge(s["rows_in"], 32 * (k + 1))
                dve.wait_ge(s["rt"], NU * k)
                link(v.tensor_copy(rows_f[:, 0:(NC - 1) * P], rows_i[:, 0:(NC - 1) * P]))
                v.tensor_copy(rows_f[0:RL, (NC - 1) * P:NC * P],
                              rows_i[0:RL, (NC - 1) * P:NC * P]).then_inc(s["rf"], 1)
            dve.wait_ge(s["load"], 16 * 15)
            link(v.tensor_tensor(w1[0:D, 0:D], w1[0:D, 0:D], w1[0:D, D:2 * D], ALU.subtract))
            for k in range(2):
                link(v.tensor_tensor(attb[:, k, :], attb[:, k, :], wsb[:, :], ALU.mult))
                link(v.tensor_reduce(va[:, k * H:(k + 1) * H],
                                     attb[:, k, :].rearrange("p (h d) -> p h d", h=H), AX.X, ALU.add))
            dve.wait_ge(s["cst"], 2)
            with dve.Fori(0, NB // 2) as k:
                dve.wait_ge(tab0["m"], k)
                v.tensor_copy(st2[:, :, 0:D], x0[:, ds(k * 2, 2), :]).then_inc(tab0["st"], 1)
                dve.wait_ge(tab0["m"], k + 1)
                pv = ps[5][:, 0:4 * D].rearrange("p (b c) -> p b c", b=2)
                v.tensor_copy(pt[:, ds(k * 2, 2), :], pv[:, :, 0:D])
                v.tensor_copy(qst[:, ds(k * 2, 2), :], pv[:, :, D:2 * D]).then_inc(tab0["v"], 1)

            def hv(ap, h):
                return ap[:, h * 4:(h + 1) * 4, :]

            def onehot(l, sn, r, b, half):
                m = L[l]
                dve.wait_ge(m["U"], sn)
                v.tensor_scalar(rel[:, :], dstc[:, half, ds(r * TG, TG)], blk[:, ds(b, 1)], None,
                                ALU.subtract).then_inc(m["rel"], 1)
                dve.wait_ge(m["rel"], sn + 1)
                for h in range(2):
                    v.tensor_tensor(hv(S, h), iota[:, :].unsqueeze(1).to_broadcast([P, 4, P]),
                                    rel[:, h * 4:h * 4 + 4].unsqueeze(2).to_broadcast([P, 4, P]),
                                    ALU.is_equal).then_inc(m["S"], 1)

            def steps0(i, q, half):
                m = L[0]
                dve.wait_ge(dst_in[half], (q + 1) * 16)
                def step(sn, r, b):
                    onehot(0, sn, r, b, half)
                    for h in range(2):
                        dve.wait_ge(m["az"], sn * 2 + (h + 1))
                        v.tensor_tensor(hv(h1, h)[:, :, 0:D],
                                        ps[2 + h][:, 0:256].rearrange("p (t d) -> p t d", d=D),
                                        hv(az1, h), ALU.max).then_inc(m["h"], 1)
                    for h in range(2):
                        dve.wait_ge(m["az2"], sn * 2 + (h + 1))
                        v.tensor_tensor(hv(h2, h),
                                        ps[4 + h][:, 0:256].rearrange("p (t d) -> p t d", d=D),
                                        hv(az2, h), ALU.max).then_inc(m["h2"], 1)
                    dve.wait_ge(m["U"], sn + 1)
                    dve.wait_ge(m["acc"], sn)
                    v.tensor_tensor(acc0[:, ds(b, 1), :], acc0[:, ds(b, 1), :],
                                    ps[6][:, 0:D].unsqueeze(1), ALU.add).then_inc(m["acc"], 1)
                steps(dve, i, step)
                dve.sem_inc(free_d, 1)

            link(v.memset(h1[:, :, D:D + 1], 1.0))
            dve.sem_inc(free_d, 1)
            supers(dve, steps0)

            dve.wait_ge(L[0]["acc"], G + NB - 1)

            def norm(first, y, o):
                base = first
                with dve.Fori(0, NCH) as c:
                    yy = y(c)
                    mm = mean[:, ds(c * BC, BC)]
                    vv = var[:, ds(c * BC, BC)]
                    k = [0]

                    def lk(ins):
                        k[0] += 1
                        ins.then_inc(lnv, 1)
                        dve.wait_ge(lnv, c * LN_OPS + (base * NCH * LN_OPS + k[0]))
                    if first == 0:
                        lk(v.tensor_tensor(yy, yy, acc0[:, ds(c * BC, BC), :], ALU.add))
                    else:
                        lk(v.memset(dum[:, :], 0.0))
                    lk(v.tensor_reduce(mm, yy, AX.X, ALU.add))
                    lk(v.tensor_scalar(mm, mm, 1.0 / D, None, ALU.mult))
                    lk(v.tensor_tensor(yy, yy, mm.unsqueeze(2).to_broadcast([P, BC, D]), ALU.subtract))
                    lk(v.tensor_tensor(ln_t, yy, yy, ALU.mult))
                    lk(v.tensor_reduce(vv, ln_t, AX.X, ALU.add))
                    v.tensor_scalar(vv, vv, 1.0 / D, EPS, ALU.mult, ALU.add).then_inc(lna, 1)
                    dve.wait_ge(lna, c * 2 + (base * 2 * NCH + 2))
                    apart(dve)
                    lk(v.reciprocal(vv, vv))
                    lk(v.tensor_tensor(o(c), yy, vv.unsqueeze(2).to_broadcast([P, BC, D]), ALU.mult))

            norm(0, lambda c: x0[:, ds(c * BC, BC), :], lambda c: x1[:, ds(c * BC, BC), 0:D])

            with dve.Fori(0, NB // 2) as k:
                dve.wait_ge(tab1["m"], k)
                v.tensor_copy(st2[:, :, 0:D], x1[:, ds(k * 2, 2), 0:D]).then_inc(tab1["st"], 1)
                dve.wait_ge(tab1["m"], k + 1)
                pv = ps[5][:, 0:4 * H].rearrange("p (b c) -> p b c", b=2)
                v.tensor_copy(x1[:, ds(k * 2, 2), D:XW], pv[:, :, 0:H]).then_inc(tab1["v"], 1)
                v.tensor_copy(adst[:, ds(k * 2, 2), :], pv[:, :, H:2 * H]).then_inc(tab1["v"], 1)
            dve.wait_ge(tab1["v"], 2 * (NB // 2))
            link(v.tensor_tensor(Mx[:, :, :], x1[:, :, D:XW], adst[:, :, :], ALU.add))
            link(v.scalar_tensor_tensor(Mx[:, :, :], Mx[:, :, :], 0.2, Mx[:, :, :], ALU.mult, ALU.max))
            for h in range(H):
                v.tensor_copy(acc[:, :, h, 0:D], x1[:, :, 0:D])
            link(v.memset(acc[:, :, :, D:D + 1], 1.0))

            def steps1(i, q, half):
                m = L[1]
                dve.wait_ge(gath[1][half], q * (16 * TS) + 16 * TS)
                gt = g1[:, half * TS:(half + 1) * TS, D:XW].rearrange("p (g j) h -> p j h g", j=TG)
                for h in range(H):
                    a = v.tensor_copy(edgeA[:, :, h * GS:(h + 1) * GS], gt[:, :, h, :])
                a.then_inc(sgv, 1)
                dve.wait_ge(row_in, i * (16 * H) + 16 * H)
                dve.wait_ge(sgp, i * 3 + 1)
                def lk(n, ins):
                    ins.then_inc(m["dv"], 1)
                    dve.wait_ge(m["dv"], i * 7 + n)
                lk(1, v.tensor_tensor(rowR[:, 1:GE], rowD[:, 1:GE], rowD[:, 0:GE - 1], ALU.not_equal))
                lk(2, v.tensor_scalar(rowR[:, 1:GE], rowR[:, 1:GE], -BIG, None, ALU.mult))
                for h in range(2):
                    lk(3 + h, v.tensor_tensor_scan(rowF[:, h * 512:h * 512 + 512], rowR[:, h * 512:h * 512 + 512],
                                                   ps[h][0:32, :],
                                                   -BIG if h == 0 else rowF[:, 511:512], ALU.add, ALU.max))
                rowM = rowD[:, :].bitcast(f32)
                v.tensor_tensor_scan(rowM[:, ::-1], rowR[:, 1:GE + 1][:, ::-1], rowF[:, ::-1],
                                     -BIG, ALU.add, ALU.max).then_inc(sgv, 1)
                dve.wait_ge(sgv, i * 4 + 2)
                v.tensor_scalar(rowF[0:GS, :], rowR[0:GS, 1:GE + 1], -1.0, None, ALU.is_lt).then_inc(sgv, 1)
                dve.wait_ge(sgp, i * 3 + 2)
                eM = edgeM[:, :, :].rearrange("p (g j) h -> p j h g", j=TG)
                pm = ps[2][:, 0:TG * 32].rearrange("p (j h g) -> p j h g", j=TG, h=H)
                for h in range(H):
                    o = edgeM[:, :, h].rearrange("p (g j) -> p j g", j=TG)
                    a = v.tensor_copy(o, pm[:, :, h, :])
                lk(5, a)
                dve.wait_ge(sgp, i * 3 + 3)
                lk(6, v.tensor_copy(edgeE[:, :, H].rearrange("p (g j) -> p j g", j=TG),
                                    ps[5][:, 0:TG * GS].rearrange("p (j g) -> p j g", j=TG)))
                lk(7, v.tensor_tensor(edgeE[:, :, 0:H], edgeM[:, :, :],
                                      edgeE[:, :, H:H + 1].to_broadcast([P, TS, H]), ALU.mult))
                dve.sem_inc(sgv, 1)
                dve.wait_ge(dst_in[half], (q + 1 + (NS - NS // 2 if half == 0 else NS // 2)) * 16)

                def step(sn, r, b):
                    onehot(1, sn, r, b, half)
                    tiles = r * TG
                    v.tensor_copy(Y[:, :, UW:YW], edgeE[:, ds(tiles, TG), :])
                    dve.wait_ge(m["ad"], sn + 1)
                    K = 11
                    def l2(n, ins):
                        ins.then_inc(m["z"], 1)
                        dve.wait_ge(m["z"], sn * K + n)
                    adx = ps[2][:, 0:TG * H].rearrange("p (t h) -> p t h", h=H)
                    v.tensor_tensor(zz[:, 0], g1[:, ds(tiles + half * TS, TG), D:XW], adx, ALU.add)
                    l2(1, v.tensor_tensor(zz[:, 1], edgeM[:, ds(tiles, TG), :], adx, ALU.add))
                    l2(2, v.scalar_tensor_tensor(lz[:, :, :, :].rearrange("p a t h -> p (a t h)"),
                                                 zz[:, :, :, :].rearrange("p a t h -> p (a t h)"), 0.2,
                                                 zz[:, :, :, :].rearrange("p a t h -> p (a t h)"),
                                                 ALU.mult, ALU.max))
                    l2(3, v.tensor_tensor(dw[:, :, :], lz[:, 0], lz[:, 1], ALU.subtract))
                    dve.wait_ge(m["w"], sn + 1)
                    y4 = Y[:, :, 0:UW].rearrange("p t (h d) -> p t h d", h=H)
                    for h in range(2):
                        for t in range(h * 4, h * 4 + 4):
                            a = v.tensor_tensor(y4[:, t, :, 0:D],
                                                g1[:, ds(tiles + (half * TS + t), 1), 0:D].to_broadcast([P, H, D]),
                                                y4[:, t, :, D:D + 1].to_broadcast([P, H, D]), ALU.mult)
                        a.then_inc(m["h"], 1)
                    dve.wait_ge(m["U"], sn + 1)
                    ub = ps[6][:, 0:UW].rearrange("p (h d) -> p h d", h=H)
                    mb = Mx[:, ds(b, 1), :]
                    l2(4, v.tensor_tensor(nz[:, 0:1, :], ps[6][:, UW:UW + H].unsqueeze(1), adst[:, ds(b, 1), :], ALU.add))
                    v.tensor_scalar(pen[:, :], ps[6][:, UW + H:YW], BIG, -BIG, ALU.mult, ALU.add)
                    l2(5, v.scalar_tensor_tensor(nz[:, 1, :], nz[:, 0, :], 0.2, nz[:, 0, :], ALU.mult, ALU.max))
                    l2(6, v.tensor_scalar(nz[:, 2, :], nz[:, 1, :], pen[:, 0:1], None, ALU.add))
                    l2(7, v.tensor_tensor(mnew[:, :].unsqueeze(1), nz[:, 2:3, :], mb, ALU.max))
                    v.tensor_tensor(dd[:, 0:1, :], mb, mnew[:, :].unsqueeze(1), ALU.subtract)
                    l2(8, v.tensor_tensor(dd[:, 1, :], nz[:, 2, :], mnew[:, :], ALU.subtract))
                    apart(dve)
                    l2(9, v.tensor_copy(mb, mnew[:, :].unsqueeze(1)))
                    dve.wait_ge(m["e"], sn + 1)
                    l2(10, v.tensor_tensor(S4(), ub, ee[:, 1, :].unsqueeze(2).to_broadcast([P, H, D + 1]), ALU.mult))
                    ab = acc[:, ds(b, 1), :, :].rearrange("p b h d -> p (b h) d")
                    l2(11, v.tensor_tensor(ab, ab, ee[:, 0, :].unsqueeze(2).to_broadcast([P, H, D + 1]), ALU.mult))
                    v.tensor_tensor(ab, ab, S4(), ALU.add).then_inc(m["acc"], 1)
                    dve.wait_ge(m["acc"], sn + 1)
                steps(dve, i, step)
                dve.sem_inc(free_d, 1)
                dve.sem_inc(free_g, 1)

            def S4():
                return S[:, 0:3, :].rearrange("p t n -> p (t n)")[:, 0:UW].rearrange("p (h d) -> p h d", h=H)

            supers(dve, steps1)

            dve.wait_ge(L[1]["acc"], G + NB - 1)
            link(v.tensor_scalar(Mx[:, :, :], acc[:, :, :, D], 1e-16, None, ALU.add))
            link(v.reciprocal(Mx[:, :, :], Mx[:, :, :]))
            link(v.tensor_scalar(Mx[:, :, :], Mx[:, :, :], 1.0 / H, None, ALU.mult))
            o2 = Y[:, 0:2, 0:H * D].rearrange("p t (h d) -> p t h d", h=H)
            with dve.Fori(0, NB // 2) as k:
                dve.wait_ge(fin["m"], k)
                for t in range(2):
                    a = v.tensor_tensor(o2[:, t], acc[:, ds(k * 2 + t, 1), :, 0:D].rearrange("p b h d -> p (b h) d"),
                                        Mx[:, ds(k * 2 + t, 1), :].rearrange("p b h -> p (b h)").unsqueeze(2)
                                        .to_broadcast([P, H, D]), ALU.mult)
                a.then_inc(fin["st"], 1)
                dve.wait_ge(fin["m"], k + 1)
                v.tensor_tensor(x1[:, ds(k * 2, 2), 0:D], x1[:, ds(k * 2, 2), 0:D],
                                ps[6][:, 0:2 * D].rearrange("p (b d) -> p b d", b=2), ALU.add).then_inc(fin["v"], 1)
            dve.wait_ge(fin["v"], NB // 2)
            norm(1, lambda c: x1[:, ds(c * BC, BC), 0:D], lambda c: x1[:, ds(c * BC, BC), 0:D])

        @block.tensor
        def _(pe):
            t_ = nc.tensor
            pe.wait_ge(s["idn"], 2)
            for k in range(2):
                pe.wait_ge(s["rf"], k + 1)
                for c in range(NC):
                    n = P if c < NC - 1 else RL
                    u, j = k * NU + c // 4, c % 4
                    if j == 0 and u >= 2:
                        pe.wait_ge(s["rc"], u - 1)
                    last = t_.transpose(ps[u % 2][:, j * P:j * P + n], rows_f[0:n, c * P:c * P + P],
                                        ident[0:n, 0:n])
                    if j == 3 or c == NC - 1:
                        last.then_inc(s["rt"], 1)
            pe.wait_ge(s["load"], 16 * 15)
            with pe.Fori(0, NB // 2) as k:
                pe.wait_ge(tab0["st"], k + 1)
                for j in range(2):
                    last = t_.transpose(ps[4][0:D + 1, j * P:j * P + P], st2[:, j, :], ident[:, :])
                last.then_inc(tab0["tp"], 1)
                pe.wait_ge(tab0["tc"], k + 1)
                pe.wait_ge(tab0["v"], k)
                for j in range(2):
                    last = t_.matmul(ps[5][:, j * 2 * D:(j + 1) * 2 * D], stT[:, j, :], w1[:, :],
                                     start=True, stop=True)
                last.then_inc(tab0["m"], 1)
            pe.wait_ge(s["bt"], 1)

            def transposes(l, sn):
                m = L[l]
                for h in range(2):
                    pe.wait_ge(m["S"], sn * 2 + (h + 1))
                    for t in range(4):
                        last = t_.transpose(ps[h][:, t * P:t * P + P], S[:, h * 4 + t, :], ident[:, :])
                    last.then_inc(m["stp"], 1)

            def steps0(i, q, half):
                m = L[0]
                pe.wait_ge(gath[0][half], q * (16 * TS) + 16 * TS)
                def step(sn, r, b):
                    transposes(0, sn)
                    for h in range(2):
                        pe.wait_ge(m["sts"], sn * 2 + (h + 1))
                        t_.matmul(ps[2 + h][:, 0:256], ident[:, :],
                                  g0[:, ds(r * TG + (half * TS + 4 * h), 4), :], start=True, stop=False,
                                  skip_group_check=True)
                        for t in range(4):
                            last = t_.matmul(ps[2 + h][:, t * D:t * D + D], ST[:, h * 4 + t, :],
                                             pt[:, ds(b, 1), :], start=False, stop=(t == 3), skip_group_check=True)
                        last.then_inc(m["z"], 1)
                    for h in range(2):
                        pe.wait_ge(m["h"], sn * 2 + (h + 1))
                        for t in range(4):
                            last = t_.transpose(ps[h][0:D + 1, t * P:t * P + P], h1[:, h * 4 + t, :], ident[:, :])
                        last.then_inc(m["htp"], 1)
                    for h in range(2):
                        pe.wait_ge(m["hts"], sn * 2 + (h + 1))
                        for t in range(4):
                            last = t_.matmul(ps[4 + h][:, t * D:t * D + D], h1T[:, h * 4 + t, :],
                                             w2[:, :], start=True, stop=True)
                        last.then_inc(m["z2"], 1)
                    pe.wait_ge(m["acc"], sn)
                    for h in range(2):
                        pe.wait_ge(m["h2"], sn * 2 + (h + 1))
                        for t in range(4):
                            last = t_.matmul(ps[6][:, 0:D], S[:, h * 4 + t, :], h2[:, h * 4 + t, :],
                                             start=(h + t == 0), stop=(h * 4 + t == 7))
                    last.then_inc(m["U"], 1)
                steps(pe, i, step)
                t_.matmul(ps[7][0:1, 0:1], ones[0:1, 0:1], ones[0:1, 0:1], start=True, stop=True).then_inc(free_g, 1)

            t_.matmul(ps[7][0:1, 0:1], ones[0:1, 0:1], ones[0:1, 0:1], start=True, stop=True).then_inc(free_g, 1)
            supers(pe, steps0)

            with pe.Fori(0, NB // 2) as k:
                pe.wait_ge(tab1["st"], k + 1)
                apart(pe)
                for j in range(2):
                    last = t_.transpose(ps[4][0:D, j * P:j * P + P], st2[:, j, 0:D], ident[:, :])
                last.then_inc(tab1["tp"], 1)
                pe.wait_ge(tab1["tc"], k + 1)
                pe.wait_ge(tab1["v"], k * 2)
                for j in range(2):
                    last = t_.matmul(ps[5][:, j * 2 * H:(j + 1) * 2 * H], stT[0:D, j, :], va[:, :], start=True, stop=True)
                last.then_inc(tab1["m"], 1)

            def steps1(i, q, half):
                m = L[1]
                
                pe.wait_ge(sgv, i * 4 + 1)
                for j in range(TG):
                    last = t_.transpose(ps[j // 4][0:32, (j % 4) * P:(j % 4) * P + P], edgeA[:, j, :], ident[:, :])
                last.then_inc(sgp, 1)
                rowM = rowD[:, :].bitcast(f32)
                pe.wait_ge(sgv, i * 4 + 2)
                apart(pe)
                for j in range(TG):
                    last = t_.transpose(ps[2][:, j * 32:j * 32 + 32], rowM[:, j * P:(j + 1) * P], ident[0:32, 0:32])
                last.then_inc(sgp, 1)
                pe.wait_ge(sgv, i * 4 + 3)
                apart(pe)
                for j in range(TG):
                    last = t_.transpose(ps[5][:, j * GS:j * GS + GS], rowF[0:GS, j * P:(j + 1) * P], ident[0:GS, 0:GS])
                last.then_inc(sgp, 1)
                pe.wait_ge(sgv, i * 4 + 4)

                def step(sn, r, b):
                    transposes(1, sn)
                    for h in range(2):
                        pe.wait_ge(m["sts"], sn * 2 + (h + 1))
                        for t in range(h * 4, h * 4 + 4):
                            last = t_.matmul(ps[2][:, t * H:t * H + H], ST[:, t, :],
                                             adst[:, ds(b, 1), :], start=True, stop=True)
                    last.then_inc(m["ad"], 1)
                    pe.wait_ge(m["acc"], sn)
                    for h in range(2):
                        pe.wait_ge(m["h"], sn * 2 + (h + 1))
                        for t in range(4):
                            last = t_.matmul(ps[6][:, 0:YW], S[:, h * 4 + t, :], Y[:, h * 4 + t, :],
                                             start=(h + t == 0), stop=(h * 4 + t == 7))
                    last.then_inc(m["U"], 1)
                steps(pe, i, step)
            supers(pe, steps1)

            with pe.Fori(0, NB // 2) as k:
                pe.wait_ge(fin["st"], k + 1)
                for j in range(2):
                    for u in range(2):
                        last = t_.transpose(ps[4][:, (j * 2 + u) * P:(j * 2 + u + 1) * P],
                                            Y[:, j, u * P:u * P + P], ident[:, :])
                last.then_inc(fin["tp"], 1)
                pe.wait_ge(fin["tc"], k + 1)
                pe.wait_ge(fin["v"], k)
                for j in range(2):
                    o = ps[6][:, j * D:j * D + D]
                    t_.matmul(o, ST[:, j * 2, :], wf[:, 0, :], start=True, stop=False)
                    t_.matmul(o, ST[:, j * 2 + 1, :], wf[:, 1, :], start=False, stop=False)
                    last = t_.matmul(o, ones[:, :], biasr[:, :], start=False, stop=True)
                last.then_inc(fin["m"], 1)

        @block.scalar
        def _(act):
            a_ = nc.scalar
            with nc.allow_non_contiguous_dma(reason="one destination per group"):
                act.dma_start(Bt[0:1, 0:NG], dst.rearrange("(g e) -> g e", e=64)[0::GE // 64, 0:1]
                              .rearrange("g e -> e g")).then_inc(s["b_ld"], 16)
            for k, a in enumerate((src, dst)):
                act.wait_ge(s["rf"], k)
                act.dma_start(rows_i[:, 0:(NC - 1) * P].rearrange("p (c e) -> p c e", e=P),
                              a[0:(NC - 1) * P * P].rearrange("(c p e) -> p c e", p=P, e=P)
                              ).then_inc(s["rows_in"], 16)
                act.dma_start(rows_i[0:RL, (NC - 1) * P:NC * P],
                              a[(NC - 1) * P * P:E].rearrange("(p e) -> p e", e=P)).then_inc(s["rows_in"], 16)
            for k, table in enumerate((srcT, dstT)):
                for q in range(NU):
                    act.wait_ge(s["rt"], k * NU + q + 1)
                    n = min(4 * P, NT - q * 4 * P)
                    a_.copy(table[:, q * 4 * P:q * 4 * P + n], ps[(k * NU + q) % 2][:, 0:n]).then_inc(s["rc"], 1)

            def copied(m, rows):
                with act.Fori(0, NB // 2) as k:
                    act.wait_ge(m["tp"], k + 1)
                    a_.copy(stT[0:rows, :, :], ps[4][0:rows, 0:2 * P].rearrange("p (a b) -> p a b", a=2)
                            ).then_inc(m["tc"], 1)

            copied(tab0, D + 1)
            act.wait_ge(s["bt"], 1)

            def to_sbuf(m, sn):
                for h in range(2):
                    act.wait_ge(m["stp"], sn * 2 + (h + 1))
                    a_.copy(ST[:, h * 4:h * 4 + 4, :], ps[h][:, :].rearrange("p (t n) -> p t n", t=4)
                            ).then_inc(m["sts"], 1)

            def steps0(i, q, half):
                m = L[0]
                def step(sn, r, b):
                    to_sbuf(m, sn)
                    for h in range(2):
                        act.wait_ge(m["z"], sn * 2 + (h + 1))
                        a_.mul(az1[:, h * 4:h * 4 + 4, :],
                               ps[2 + h][:, 0:256].rearrange("p (t d) -> p t d", d=D), 0.01
                               ).then_inc(m["az"], 1)
                    for h in range(2):
                        act.wait_ge(m["htp"], sn * 2 + (h + 1))
                        a_.copy(h1T[:, h * 4:h * 4 + 4, :],
                                ps[h][0:D + 1, :].rearrange("p (t n) -> p t n", t=4)).then_inc(m["hts"], 1)
                    for h in range(2):
                        act.wait_ge(m["z2"], sn * 2 + (h + 1))
                        a_.mul(az2[:, h * 4:h * 4 + 4, :],
                               ps[4 + h][:, 0:256].rearrange("p (t d) -> p t d", d=D), 0.01
                               ).then_inc(m["az2"], 1)
                steps(act, i, step)
            supers(act, steps0)

            def roots(base):
                with act.Fori(0, NCH) as c:
                    act.wait_ge(lna, c * 2 + (base * 2 * NCH + 1))
                    vv = var[:, ds(c * BC, BC)]
                    a_.activation(vv, vv, ACT.Sqrt).then_inc(lna, 1)

            roots(0)
            copied(tab1, D)

            def steps1(i, q, half):
                m = L[1]
                def step(sn, r, b):
                    to_sbuf(m, sn)
                    act.wait_ge(m["z"], sn * 11 + 3)
                    y4 = Y[:, :, 0:UW].rearrange("p t (h d) -> p t h d", h=H)
                    a_.activation(y4[:, :, :, D], dw[:, :, :], ACT.Exp).then_inc(m["w"], 1)
                    act.wait_ge(m["z"], sn * 11 + 9)
                    a_.activation(ee[:, :, :], dd[:, :, :], ACT.Exp).then_inc(m["e"], 1)
                steps(act, i, step)
            supers(act, steps1)

            with act.Fori(0, NB // 2) as k:
                act.wait_ge(fin["tp"], k + 1)
                a_.copy(ST[:, 0:4, :], ps[4][:, :].rearrange("p (t n) -> p t n", t=4)).then_inc(fin["tc"], 1)
            roots(1)


_IN = ["x", "src", "dst", "L0_gnn_W1", "L0_gnn_b1", "L0_gnn_W2", "L0_gnn_b2", "L1_gnn_W", "L1_gnn_att_src",
       "L1_gnn_att_dst", "L1_gnn_bias"]


def kernel(**inputs):
    import numpy as _np
    import concourse.bacc as _bacc
    from concourse import mybir as _mybir
    from concourse.bass_utils import run_bass_kernel_spmd as _run

    nc = _bacc.Bacc("TRN2", target_bir_lowering=False, num_devices=1)
    f32, i32 = _mybir.dt.float32, _mybir.dt.int32
    arrays, args = {}, []
    for name in _IN:
        a = _np.ascontiguousarray(inputs[name])
        arrays["in_" + name] = a
        args.append(nc.dram_tensor("in_" + name, a.shape, _mybir.dt.from_np(a.dtype), kind="ExternalInput").ap())
    args.append(nc.dram_tensor("out_0", (N, D), f32, kind="ExternalOutput").ap())
    for name, shape, dt in (("q_dram", (NB * P, D), f32), ("x_dram", (NB * P, XW), f32),
                            ("srcT_dram", (P, T), i32), ("dstT_dram", (P, T), f32), ("dst_dram", (EP,), i32)):
        args.append(nc.dram_tensor(name, shape, dt, kind="Internal").ap())
    build(nc, *args)
    r = _run(nc, [arrays], core_ids=[0])
    return r.results[0]["out_0"]
```

```python
import concourse.bass as bass
from concourse import mybir
from contextlib import ExitStack

N, E, D, H = 12500, 400000, 64, 4
P = 128
NB = -(-N // P)
LAST = N - (NB - 1) * P
TG = 8
GE = TG * P
GS = 8
TS = TG * GS
NT = E // P
NG = -(-E // GE)
NS = -(-NG // GS)
G = NS * GS
T = G * TG
EP = T * P
XW = D + H
UW = H * (D + 1)
YW = UW + H + 1
BIG = 1.0e30
STEPS = G + NB - 1
PAST = GS + 3
BF = 3 * D
PADNODE = 1000000
NC = -(-NT // P)
RL = NT - (NC - 1) * P
NU = -(-NC // 4)
NCH = 7
BC = NB // NCH
LN_OPS = 7
EPS = 1e-5


def build(nc, x, src, dst, W1, b1, W2, b2, W, att_src, att_dst, bias, out, q_dram, x_dram, srcT_dram,
          dstT_dram, dst_dram):
    f32, i32, bf16 = mybir.dt.float32, mybir.dt.int32, mybir.dt.bfloat16
    ALU, ACT, AX = mybir.AluOpType, mybir.ActivationFunctionType, mybir.AxisListType
    ds = bass.ds
    ctx = ExitStack()
    with ctx:
        def sb(name, shape, dt=f32):
            return ctx.enter_context(nc.sbuf_tensor(name, shape, dt))

        def sem(name):
            return ctx.enter_context(nc.semaphore(name))

        state = sb("state", [P, NB * UW])
        big = sb("big", [P, 2 * TS * XW + NB * XW])
        x1 = big[:, 2 * TS * XW:].rearrange("p (b d) -> p b d", d=XW)
        S = sb("S", [P, 4 * TG, P], bf16)
        ST = sb("ST", [P, TG, P], bf16)
        Y = sb("Y", [P, TG, YW])
        rowD = sb("rowD", [32, GE], i32)
        rowX = sb("rowX", [P, GE + 1])
        rowR = rowX[0:32, :]
        rowA = sb("rowA", [P, GE])
        rowF = rowA[0:32, :]
        idx = sb("idx", [P, 2, TS], i32)
        dstc = sb("dstc", [P, 2, TS])
        edgeM = sb("edgeM", [P, 2 * TS, H])
        edgeE = sb("edgeE", [P, 2 * TS, H + 1])
        edgeA = sb("edgeA", [P, TG, 32])
        ident = sb("ident", [P, P])
        identb = sb("identb", [P, P], bf16)
        iotaf = rowX[:, 0:P]
        iota = sb("iota", [P, P], bf16)
        blk = sb("blk", [P, NB])
        Bt = sb("Bt", [1, GS + G + 1], i32)
        rel = sb("rel", [P, TG], bf16)
        adst = sb("adst", [P, NB, H])
        adp = sb("adp", [P, NB, 3, H], bf16)
        Mx = sb("Mx", [P, NB, H])
        adx = sb("adx", [P, TG, H])
        zz = sb("zz", [P, 2, TG, H])
        lz = sb("lz", [P, 2, TG, H])
        dw = sb("dw", [P, TG, H])
        wb = sb("wb", [P, TG, H])
        nz = sb("nz", [P, 3, H])
        pen = sb("pen", [P, 1])
        mnew = sb("mnew", [P, H])
        dd = sb("dd", [P, 2, H])
        ee = sb("ee", [P, 2, H])
        Tm = sb("Tm", [P, H, D + 1])
        wf = sb("wf", [P, 2, D])
        biasr = sb("biasr", [1, D])
        ones = rowX[0:1, 0:P]
        wsb = rowA[0:D, 0:H * D]
        attb = rowA[0:D, H * D:3 * H * D].rearrange("p (a c) -> p a c", a=2)
        w1 = rowA[0:D + 1, 3 * H * D:3 * H * D + 2 * D]
        va = rowA[0:D, 3 * H * D + 2 * D:3 * H * D + 2 * D + 2 * H]
        mv = edgeA[:, :, :].rearrange("p j c -> p (j c)")
        mean, var = mv[:, 0:NB], mv[:, NB:2 * NB]
        em = edgeM[:, :, :].rearrange("p t h -> p (t h)")
        ee_ = edgeE[:, :, :].rearrange("p t h -> p (t h)")
        stT = em[0:D + 1, 0:2 * P].rearrange("p (a b) -> p a b", a=2)
        b2q = em[0:3, 2 * P:2 * P + TG * D // 2].bitcast(bf16)
        st2 = ee_[:, 0:2 * D + 2].rearrange("p (b d) -> p b d", b=2)
        w2d = ee_[:, 2 * D + 2:4 * D + 2]
        onesb = ee_[0:3, 4 * D + 2:4 * D + 2 + P // 2].bitcast(bf16)
        yf = Y[:, :, :].rearrange("p t d -> p (t d)")
        b2r = yf[0:1, 0:2 * TG * D].rearrange("p (a c) -> p a c", a=2)
        b2p = yf[0:1, 2 * TG * D:2 * TG * D + 3 * TG * D // 2].bitcast(bf16).rearrange("p (k c) -> p k c", k=3)

        ps = [ctx.enter_context(nc.psum_tensor(f"ps{i}", [P, 512], f32)) for i in range(8)]

        x0 = state[:, 0:NB * D].rearrange("p (b d) -> p b d", d=D)
        pq = state[:, NB * D:4 * NB * D].bitcast(bf16).rearrange("p (b k c) -> p b k c", k=3, c=2 * D)
        acc = state[:, :].rearrange("p (b h d) -> p b h d", h=H, d=D + 1)
        g0 = big[:, 0:TS * BF].bitcast(bf16).rearrange("p (t k d) -> p t k d", k=3, d=D)
        g0r = big[:, 0:TS * BF].bitcast(bf16).rearrange("p (t d) -> p t d", d=BF)
        g1 = big[:, 0:2 * TS * XW].rearrange("p (t d) -> p t d", d=XW)
        Yf = Y[:, :, :].rearrange("p t d -> p (t d)")
        h1 = Yf[:, 0:TG * D].rearrange("p (t d) -> p t d", d=D)
        az1 = Yf[:, TG * D:2 * TG * D].rearrange("p (t d) -> p t d", d=D)
        az2 = Yf[:, 2 * TG * D:3 * TG * D]
        h2 = Yf[:, 3 * TG * D:4 * TG * D]
        h2p = rowX[:, 0:3 * TG * D // 2].bitcast(bf16).rearrange("p (k c) -> p k c", k=3)
        h1T = rowA[:, 0:4 * P].rearrange("p (t e) -> p t e", e=P)
        Sf = S[:, 2 * TG:4 * TG, :].rearrange("p t n -> p (t n)").bitcast(f32).rearrange("p (t n) -> p t n", n=P)
        rows_i = big[:, 0:NC * P].bitcast(i32)
        rows_f = big[:, NC * P:2 * NC * P]
        srcT = big[:, 2 * NC * P:2 * NC * P + T].bitcast(i32)
        dstT = big[:, 2 * NC * P + T:2 * NC * P + 2 * T]
        ln_t = big[:, 0:BC * D].rearrange("p (b d) -> p b d", d=D)
        res = rowX[:, 0:4 * D].rearrange("p (b c) -> p b c", b=2)

        names = "idb b2 b2in load clr pad cst idn b_ld bt rows_in rf rt rc q_out t_out d_out".split()
        s = {n: sem("s_" + n) for n in names}
        idx_in = [sem("idx_in0"), sem("idx_in1")]
        dst_in = [sem("dst_in0"), sem("dst_in1")]
        gath = [[sem(f"gath{l}{p}") for p in range(2)] for l in range(2)]
        row_in = sem("row_in")
        free_d = sem("free_d")
        gdone = sem("gdone")
        STAGES = [{"rel": (1, 0), "S": (2, 0), "stp": (2, 0), "sts": (2, 0), "z": (2, 0), "az": (2, 0),
                   "h": (2, -1), "htp": (2, -1), "hts": (2, -1), "z2": (1, -1), "az2": (1, -1),
                   "h2": (1, -2), "hi": (1, -1), "rest": (1, -2), "mid": (1, -1), "lo": (1, -2),
                   "U": (1, -2), "acc": (1, -3)},
                  {"rel": (1, 0), "S": (2, 0), "stp": (2, 0), "sts": (2, 0), "ad": (1, 0), "zc": (4, -1),
                   "w": (1, -1), "sf": (2, 0), "y": (2, -1), "U": (2, -1), "mg": (7, -2), "e": (1, -2),
                   "tm": (1, -2), "acc": (1, -2)}]
        L = [{n: sem(f"l{l}_{n}") for n in STAGES[l]} for l in range(2)]

        def done(eng, l, n, sn, back, part=None):
            k = STAGES[l][n][0]
            eng.wait_ge(L[l][n], sn * k + (k * (PAST - back) + (k if part is None else part)))

        def prime(eng, l, names):
            for n in names.split():
                k, first = STAGES[l][n]
                eng.sem_inc(L[l][n], k * (first + PAST))

        spl = sem("split")
        clean = sem("clean")
        dvs = sem("sg_chain")
        sgp, sgv = sem("sg_pe"), sem("sg_dve")
        lnv = sem("ln_dve")
        lna = sem("ln_act")
        vch = sem("dve_chain")
        tab0, tab1, fin = [{n: sem(f"{t}_{n}") for n in "st tp tc m v".split()}
                           for t in ("tab0", "tab1", "fin")]
        idle = sem("idle")
        x_out = sem("x_out")
        o_out = sem("o_out")

        block = ctx.enter_context(nc.Block())

        def supers(eng, body):
            with eng.Fori(0, NS // 2) as q:
                body(q * 2, q, 0)
                body(q * 2 + 1, q, 1)
            if NS % 2:
                body(NS - 1, NS // 2, 0)

        def apart(eng):
            eng.sem_inc(idle, 1)

        def steps(eng, i, step):
            apart(eng)
            with eng.Fori(0, GS) as r:
                g = i * GS + r
                b0 = eng.value_load(Bt[0:1, ds(g + GS, 1)], min_val=0, max_val=NB - 1)
                b1 = eng.value_load(Bt[0:1, ds(g + (GS + 1), 1)], min_val=0, max_val=NB - 1)
                with eng.Fori(b0, b1 + 1) as b:
                    step(g + b, r, b)

        @block.sync
        def _(sp):
            xr = x[0:(NB - 1) * P, :].rearrange("(b p) d -> p b d", p=P)
            sp.wait_ge(s["clr"], 1)
            sp.dma_start(x0[:, 0:NB - 1, :], xr).then_inc(s["load"], 16)
            sp.dma_start(x0[0:LAST, NB - 1, :], x[(NB - 1) * P:N, :]).then_inc(s["load"], 16)
            sp.dma_start(w1[0:D, 0:D], W1[0:D, :]).then_inc(s["load"], 16)
            sp.dma_start(w1[0:D, D:2 * D], W1[D:2 * D, :]).then_inc(s["load"], 16)
            sp.dma_start(w1[D:D + 1, 0:D], b1.rearrange("(a d) -> a d", a=1)).then_inc(s["load"], 16)
            for h in range(2):
                sp.dma_start(w2d[h * D:(h + 1) * D, h * D:(h + 1) * D], W2[:, :]).then_inc(s["load"], 16)
            sp.dma_start(b2r[:, 0, 0:D], b2.rearrange("(a d) -> a d", a=1)).then_inc(s["load"], 16)
            sp.dma_start(wsb[:, :], W[:, :]).then_inc(s["load"], 16)
            sp.dma_start(attb[:, 0, :], att_src.rearrange("a h d -> a (h d)").to_broadcast([D, H * D])
                         ).then_inc(s["load"], 16)
            sp.dma_start(attb[:, 1, :], att_dst.rearrange("a h d -> a (h d)").to_broadcast([D, H * D])
                         ).then_inc(s["load"], 16)
            for h in range(H):
                sp.dma_start(wf[(h % 2) * D:(h % 2 + 1) * D, h // 2, :], W[:, h * D:(h + 1) * D]
                             ).then_inc(s["load"], 16)
            sp.dma_start(biasr[:, :], bias.rearrange("(a d) -> a d", a=1)).then_inc(s["load"], 16)
            sp.dma_start(dst_dram[0:E].rearrange("(a c) -> a c", a=16),
                         dst.rearrange("(a c) -> a c", a=16)).then_inc(s["d_out"], 16)
            sp.wait_ge(s["pad"], 1)
            sp.dma_start(dst_dram[E:EP].rearrange("(a c) -> a c", a=2),
                         rowD[0:2, 0:(EP - E) // 2]).then_inc(s["d_out"], 16)
            sp.wait_ge(s["rc"], NU)
            sp.dma_start(srcT_dram[:, :], srcT).then_inc(s["t_out"], 16)
            sp.wait_ge(s["rc"], 2 * NU)
            sp.dma_start(dstT_dram[:, :], dstT).then_inc(s["t_out"], 16)
            sp.wait_ge(s["b2"], 1)
            sp.dma_start(b2q[:, :], b2p[0:1, :, :]).then_inc(s["b2in"], 16)
            sp.wait_ge(tab0["v"], NB // 2 + 1)
            for k in range(3):
                sp.dma_start(q_dram.rearrange("(b p) d -> p b d", p=P)[:, :, k * D:(k + 1) * D],
                             pq[:, :, k, D:2 * D]).then_inc(s["q_out"], 16)
            sp.wait_ge(s["t_out"], 32)

            for l in range(2):
                def chunk(i, q, half):
                    sp.wait_ge(gdone, i + (l * NS + 1))
                    sp.dma_start(idx[:, half, :], srcT_dram[:, ds(i * TS, TS)]).then_inc(idx_in[half], 16)
                    sp.wait_ge(free_d, i + (l * NS + 1))
                    sp.dma_start(dstc[:, half, :], dstT_dram[:, ds(i * TS, TS)]).then_inc(dst_in[half], 16)
                    if l:
                        sp.wait_ge(sgv, i * 4 + 1)
                        for h in range(H):
                            sp.dma_start(rowD[h * GS:(h + 1) * GS, :],
                                         dst_dram[ds(i * (GS * GE), GS * GE)].rearrange("(g e) -> g e", g=GS)
                                         ).then_inc(row_in, 16)
                if l:
                    sp.wait_ge(s["d_out"], 32)
                supers(sp, chunk)
                if l == 0:
                    sp.wait_ge(tab1["v"], 2 * (NB // 2) + 1)
                    sp.dma_start(x_dram.rearrange("(b p) d -> p b d", p=P), x1).then_inc(x_out, 16)
            sp.wait_ge(lnv, 2 * NCH * LN_OPS)
            sp.dma_start(out[0:(NB - 1) * P, :].rearrange("(b p) d -> p b d", p=P),
                         x1[:, 0:NB - 1, 0:D]).then_inc(o_out, 16)
            sp.dma_start(out[(NB - 1) * P:N, :], x1[0:LAST, NB - 1, 0:D]).then_inc(o_out, 16)
            sp.wait_ge(o_out, 32)

        @block.gpsimd
        def _(pool):
            nc.gpsimd.iota(iotaf[:, :], [[1, P]], base=0, channel_multiplier=0,
                           allow_small_or_imprecise_dtypes=True).then_inc(s["cst"], 1)
            nc.gpsimd.iota(blk[:, :], [[P, NB]], base=0, channel_multiplier=0,
                           allow_small_or_imprecise_dtypes=True).then_inc(s["cst"], 1)
            nc.gpsimd.memset(ident[:, :], 0.0).then_inc(s["idn"], 1)
            pool.wait_ge(s["idn"], 1)
            nc.gpsimd.affine_select(out=ident[:, :], in_=ident[:, :], compare_op=ALU.not_equal, fill=1.0,
                                    base=0, pattern=[[-1, P]], channel_multiplier=1).then_inc(s["idn"], 1)
            for l in range(2):
                if l == 0:
                    pool.wait_ge(s["q_out"], 48)
                    pool.wait_ge(s["bt"], 2)
                    pool.wait_ge(s["t_out"], 32)
                else:
                    pool.wait_ge(x_out, 16)

                def gathers(i, q, half):
                    n = q + 1 + (0 if l == 0 else (NS - NS // 2 if half == 0 else NS // 2))
                    pool.wait_ge(idx_in[half], n * 16)
                    gone = pool.value_load(Bt[0:1, ds(i * GS, 1)], min_val=0, max_val=NB - 1)
                    pool.wait_ge(L[l]["y" if l else "z"], (i * GS + gone) * 2 + 2 * (PAST - GS))
                    apart(pool)
                    for t in range(TS):
                        o = (g1 if l else g0r)[:, half * TS + t, :]
                        nc.gpsimd.indirect_dma_start(
                            o, None, x_dram if l else q_dram,
                            bass.IndirectOffsetOnAxis(ap=idx[:, half, t:t + 1], axis=0)
                        ).then_inc(gath[l][half], 16)
                supers(pool, gathers)

        @block.vector
        def _(dve):
            v = nc.vector
            count = [0]

            def link(ins):
                count[0] += 1
                ins.then_inc(vch, 1)
                dve.wait_ge(vch, count[0])

            link(v.memset(x0[:, NB - 1, :], 0.0))
            link(v.memset(onesb[:, :], 1.0))
            link(v.memset(w2d[:, :], 0.0))
            v.memset(w1[D:D + 1, D:2 * D], 0.0).then_inc(s["clr"], 1)
            v.memset(rowD[:, :], PADNODE).then_inc(s["pad"], 1)
            link(v.memset(st2[:, :, D:D + 1], 1.0))
            link(v.memset(S[:, :, :], 0.0))
            for t in (tab0, tab1, fin):
                dve.sem_inc(t["m"], 1)
                dve.sem_inc(t["v"], 1)
            dve.sem_inc(sgv, 1)
            link(v.memset(srcT[:, NT:T], 0))
            link(v.memset(dstT[:, NT:T], float(PADNODE)))
            dve.wait_ge(s["b_ld"], 16)
            v.memset(Bt[0:1, 0:GS], 0).then_inc(s["bt"], 1)
            link(v.tensor_scalar(Bt[0:1, GS:GS + NG], Bt[0:1, GS:GS + NG], 7, None, ALU.arith_shift_right))
            v.memset(Bt[0:1, GS + NG:GS + G + 1], NB - 1).then_inc(s["bt"], 1)
            for k in range(2):
                dve.wait_ge(s["rows_in"], 32 * (k + 1))
                if k:
                    dve.wait_ge(s["rt"], NU)
                link(v.tensor_copy(rows_f[:, 0:(NC - 1) * P], rows_i[:, 0:(NC - 1) * P]))
                v.tensor_copy(rows_f[0:RL, (NC - 1) * P:NC * P],
                              rows_i[0:RL, (NC - 1) * P:NC * P]).then_inc(s["rf"], 1)
            dve.wait_ge(s["load"], 16 * 16)
            link(v.tensor_tensor(w1[0:D, 0:D], w1[0:D, 0:D], w1[0:D, D:2 * D], ALU.subtract))
            for k in range(2):
                link(v.tensor_tensor(attb[:, k, :], attb[:, k, :], wsb[:, :], ALU.mult))
                link(v.tensor_reduce(va[:, k * H:(k + 1) * H],
                                     attb[:, k, :].rearrange("p (h d) -> p h d", h=H), AX.X, ALU.add))
            link(v.tensor_copy(b2r[:, 1, :].rearrange("p (t d) -> p t d", d=D),
                               b2r[:, 0:1, 0:D].to_broadcast([1, TG, D])))
            link(v.tensor_copy(b2p[:, 0, :], b2r[:, 1, :]))
            link(v.tensor_tensor(b2r[:, 1, :], b2r[:, 1, :], b2p[:, 0, :], ALU.subtract))
            link(v.tensor_copy(b2p[:, 1, :], b2r[:, 1, :]))
            v.tensor_tensor(b2p[:, 2, :], b2r[:, 1, :], b2p[:, 1, :], ALU.subtract).then_inc(s["b2"], 1)
            dve.wait_ge(s["cst"], 2)
            dve.wait_ge(s["idn"], 2)
            link(v.tensor_copy(iota[:, :], iotaf[:, :]))
            v.tensor_copy(identb[:, :], ident[:, :]).then_inc(s["idb"], 1)
            with dve.Fori(0, NB // 2) as k:
                dve.wait_ge(tab0["m"], k + 1)
                v.tensor_copy(st2[:, :, 0:D], x0[:, ds(k * 2, 2), :]).then_inc(tab0["st"], 1)
                dve.wait_ge(tab0["m"], k + 2)
                pv = ps[5][:, 0:4 * D].rearrange("p (b c) -> p b c", b=2)

                def part(n):
                    return pq[:, ds(k * 2, 2), n, :]

                def split(n, ins):
                    ins.then_inc(spl, 1)
                    dve.wait_ge(spl, k * 3 + n)
                split(1, v.tensor_copy(part(0), pv))
                split(2, v.tensor_tensor(res, pv, part(0), ALU.subtract))
                split(3, v.tensor_copy(part(1), res))
                v.tensor_tensor(part(2), res, part(1), ALU.subtract).then_inc(tab0["v"], 1)

            def hv(ap, h):
                return ap[:, h * 4:(h + 1) * 4, :]

            def onehot(l, sn, r, b, half, buf):
                done(dve, l, "S", sn, 1)
                v.tensor_scalar(rel[:, :], dstc[:, half, ds(r * TG, TG)], blk[:, ds(b, 1)], None,
                                ALU.subtract).then_inc(L[l]["rel"], 1)
                done(dve, l, "rel", sn, 0)
                for h in range(2):
                    v.tensor_tensor(S[:, ds(buf + 4 * h, 4), :],
                                    iota[:, :].unsqueeze(1).to_broadcast([P, 4, P]),
                                    rel[:, h * 4:h * 4 + 4].unsqueeze(2).to_broadcast([P, 4, P]),
                                    ALU.is_equal).then_inc(L[l]["S"], 1)

            class Past:
                def __init__(self, name, n, top):
                    self.regs, self.top = [dve.alloc_register(f"{name}{j}") for j in range(n)], top
                    for x in self.regs:
                        dve.reg_mov(x, 0)

                def back(self, n):
                    return dve.snap(self.regs[n - 1], min_val=0, max_val=self.top)

                def push(self, value):
                    for a, b in zip(self.regs[::-1], self.regs[-2::-1]):
                        dve.reg_mov(a, b)
                    dve.reg_mov(self.regs[0], value)

            def leaky1(sn, back):
                m = L[0]
                for h in range(2):
                    done(dve, 0, "az", sn, back, h + 1)
                    v.tensor_tensor(hv(h1, h), ps[4 + h][:, 0:256].rearrange("p (t d) -> p t d", d=D),
                                    hv(az1, h), ALU.max).then_inc(m["h"], 1)

            def add0(sn, back, b):
                done(dve, 0, "U", sn, back)
                done(dve, 0, "acc", sn, back + 1)
                v.tensor_tensor(x0[:, ds(b, 1), :], x0[:, ds(b, 1), :],
                                ps[6][:, 0:D].unsqueeze(1), ALU.add).then_inc(L[0]["acc"], 1)

            def leaky2(sn, back):
                m = L[0]
                done(dve, 0, "az2", sn, back)
                v.tensor_tensor(h2, ps[7][:, :], az2, ALU.max).then_inc(m["h2"], 1)
                done(dve, 0, "h2", sn, back)
                done(dve, 0, "hi", sn, back)
                v.tensor_tensor(h2, h2, h2p[:, 0, :], ALU.subtract).then_inc(m["rest"], 1)
                done(dve, 0, "rest", sn, back)
                done(dve, 0, "mid", sn, back)
                v.tensor_tensor(h2p[:, 2, :], h2, h2p[:, 1, :], ALU.subtract).then_inc(m["lo"], 1)

            blocks = Past("block", 3, NB - 1)

            def steps0(i, q, half):
                dve.wait_ge(dst_in[half], (q + 1) * 16)
                def step(sn, r, b):
                    onehot(0, sn, r, b, half, (sn % 4) * TG)
                    leaky1(sn, 1)
                    add0(sn, 3, blocks.back(3))
                    leaky2(sn, 2)
                    blocks.push(b)
                steps(dve, i, step)
                dve.sem_inc(free_d, 1)

            prime(dve, 0, "rel S h h2 rest lo acc")
            dve.sem_inc(free_d, 2)
            for n in (2, 3, 4, 5, 6, 7):
                link(v.memset(ps[n][:, :], 0.0))
            link(v.memset(rowX[:, :], 0.0))
            dve.wait_ge(s["b2in"], 16)
            link(v.memset(Y[:, :, :], 0.0))
            dve.sem_inc(clean, 1)
            supers(dve, steps0)
            leaky1(STEPS, 1)
            add0(STEPS, 3, blocks.back(3))
            leaky2(STEPS, 2)
            add0(STEPS + 1, 3, blocks.back(2))
            leaky2(STEPS + 1, 2)
            add0(STEPS + 2, 3, blocks.back(1))
            done(dve, 0, "acc", STEPS - 1, 0)

            def norm(first, y, o):
                base = first
                with dve.Fori(0, NCH) as c:
                    yy = y(c)
                    mm = mean[:, ds(c * BC, BC)]
                    vv = var[:, ds(c * BC, BC)]
                    k = [0]

                    def lk(ins):
                        k[0] += 1
                        ins.then_inc(lnv, 1)
                        dve.wait_ge(lnv, c * LN_OPS + (base * NCH * LN_OPS + k[0]))
                    lk(v.tensor_reduce(mm, yy, AX.X, ALU.add))
                    lk(v.tensor_scalar(mm, mm, 1.0 / D, None, ALU.mult))
                    lk(v.tensor_tensor(yy, yy, mm.unsqueeze(2).to_broadcast([P, BC, D]), ALU.subtract))
                    lk(v.tensor_tensor(ln_t, yy, yy, ALU.mult))
                    lk(v.tensor_reduce(vv, ln_t, AX.X, ALU.add))
                    v.tensor_scalar(vv, vv, 1.0 / D, EPS, ALU.mult, ALU.add).then_inc(lna, 1)
                    dve.wait_ge(lna, c * 2 + (base * 2 * NCH + 2))
                    apart(dve)
                    lk(v.reciprocal(vv, vv))
                    lk(v.tensor_tensor(o(c), yy, vv.unsqueeze(2).to_broadcast([P, BC, D]), ALU.mult))

            norm(0, lambda c: x0[:, ds(c * BC, BC), :], lambda c: x1[:, ds(c * BC, BC), 0:D])

            with dve.Fori(0, NB // 2) as k:
                dve.wait_ge(tab1["m"], k + 1)
                v.tensor_copy(st2[:, :, 0:D], x1[:, ds(k * 2, 2), 0:D]).then_inc(tab1["st"], 1)
                dve.wait_ge(tab1["m"], k + 2)
                pv = ps[5][:, 0:4 * H].rearrange("p (b c) -> p b c", b=2)
                v.tensor_copy(x1[:, ds(k * 2, 2), D:XW], pv[:, :, 0:H]).then_inc(tab1["v"], 1)
                v.tensor_copy(adst[:, ds(k * 2, 2), :], pv[:, :, H:2 * H]).then_inc(tab1["v"], 1)
            dve.wait_ge(tab1["v"], 2 * (NB // 2) + 1)
            link(v.tensor_copy(adp[:, :, 0, :], adst[:, :, :]))
            link(v.tensor_tensor(Mx[:, :, :], adst[:, :, :], adp[:, :, 0, :], ALU.subtract))
            link(v.tensor_copy(adp[:, :, 1, :], Mx[:, :, :]))
            link(v.tensor_tensor(adp[:, :, 2, :], Mx[:, :, :], adp[:, :, 1, :], ALU.subtract))
            link(v.tensor_tensor(Mx[:, :, :], x1[:, :, D:XW], adst[:, :, :], ALU.add))
            link(v.scalar_tensor_tensor(Mx[:, :, :], Mx[:, :, :], 0.2, Mx[:, :, :], ALU.mult, ALU.max))
            for h in range(H):
                v.tensor_copy(acc[:, :, h, 0:D], x1[:, :, 0:D])
            link(v.memset(acc[:, :, :, D:D + 1], 1.0))
            link(v.memset(S[:, :, :], 0.0))
            link(v.memset(rowR[:, 0:1], -BIG))
            link(v.memset(rowR[:, GE:GE + 1], -BIG))
            link(v.memset(ps[2][:, :], 0.0))
            link(v.memset(ps[6][:, :], 0.0))
            prime(dve, 1, "rel S zc y mg acc")
            dve.sem_inc(clean, 1)

            def maxima(i, q, half):
                def lk(n, ins):
                    ins.then_inc(dvs, 1)
                    dve.wait_ge(dvs, i * 7 + n)
                dve.wait_ge(gath[1][half], q * (16 * TS) + 16 * TS)
                dve.sem_inc(gdone, 1)
                gt = g1[:, half * TS:(half + 1) * TS, D:XW].rearrange("p (g j) h -> p j h g", j=TG)
                for h in range(H):
                    a = v.tensor_copy(edgeA[:, :, h * GS:(h + 1) * GS], gt[:, :, h, :])
                a.then_inc(sgv, 1)
                dve.wait_ge(row_in, i * (16 * H) + 16 * H)
                lk(1, v.tensor_tensor(rowR[:, 1:GE], rowD[:, 1:GE], rowD[:, 0:GE - 1], ALU.not_equal))
                lk(2, v.tensor_scalar(rowR[:, 1:GE], rowR[:, 1:GE], -BIG, None, ALU.mult))
                dve.wait_ge(sgp, i * 2 + 1)
                for h in range(2):
                    lk(3 + h, v.tensor_tensor_scan(rowF[:, h * 512:h * 512 + 512],
                                                   rowR[:, h * 512:h * 512 + 512], ps[3 + h][0:32, :],
                                                   -BIG if h == 0 else rowF[:, 511:512], ALU.add, ALU.max))
                rowM = rowD[:, :].bitcast(f32)
                v.tensor_tensor_scan(rowM[:, ::-1], rowR[:, 1:GE + 1][:, ::-1], rowF[:, ::-1],
                                     -BIG, ALU.add, ALU.max).then_inc(sgv, 1)
                dve.wait_ge(sgv, i * 4 + 3)
                v.tensor_scalar(rowF[0:GS, :], rowR[0:GS, 1:GE + 1], -1.0, None, ALU.is_lt).then_inc(sgv, 1)
                dve.wait_ge(sgp, i * 2 + 2)
                own = ds(half * TS, TS)
                pm = ps[5][:, 0:TG * 32].rearrange("p (j h g) -> p j h g", j=TG, h=H)
                for h in range(H):
                    a = v.tensor_copy(edgeM[:, own, h].rearrange("p (g j) -> p j g", j=TG), pm[:, :, h, :])
                lk(5, a)
                lk(6, v.tensor_copy(edgeE[:, own, H].rearrange("p (g j) -> p j g", j=TG),
                                    ps[5][:, 256:256 + TG * GS].rearrange("p (j g) -> p j g", j=TG)))
                lk(7, v.tensor_tensor(edgeE[:, own, 0:H], edgeM[:, own, :],
                                      edgeE[:, own, H:H + 1].to_broadcast([P, TS, H]), ALU.mult))
                dve.sem_inc(sgv, 1)

            def logits(sn, back, at):
                def lk(n, ins):
                    ins.then_inc(L[1]["zc"], 1)
                    if n < 4:
                        done(dve, 1, "zc", sn, back, n)
                done(dve, 1, "ad", sn, back)
                lk(1, v.tensor_reduce(adx[:, :, :],
                                      ps[2][:, 0:TG * 3 * H].rearrange("p (t k h) -> p t h k", k=3, h=H),
                                      AX.X, ALU.add))
                v.tensor_tensor(zz[:, 0], g1[:, ds(at, TG), D:XW], adx[:, :, :], ALU.add)
                lk(2, v.tensor_tensor(zz[:, 1], edgeM[:, ds(at, TG), :], adx[:, :, :], ALU.add))
                zf = zz[:, :, :, :].rearrange("p a t h -> p (a t h)")
                lk(3, v.scalar_tensor_tensor(lz[:, :, :, :].rearrange("p a t h -> p (a t h)"), zf, 0.2, zf,
                                             ALU.mult, ALU.max))
                lk(4, v.tensor_tensor(dw[:, :, :], lz[:, 0], lz[:, 1], ALU.subtract))

            def weigh(sn, back, at):
                y4 = Y[:, :, 0:UW].rearrange("p t (h d) -> p t h d", h=H)
                done(dve, 1, "w", sn, back)
                for h in range(2):
                    done(dve, 1, "U", sn, back + 1, h + 1)
                    for t in range(h * 4, h * 4 + 4):
                        v.tensor_tensor(y4[:, t, :, 0:D], g1[:, ds(at + t, 1), 0:D].to_broadcast([P, H, D]),
                                        wb[:, t, :].unsqueeze(2).to_broadcast([P, H, D]), ALU.mult)
                    v.tensor_copy(y4[:, h * 4:h * 4 + 4, :, D], wb[:, h * 4:h * 4 + 4, :])
                    v.tensor_copy(Y[:, h * 4:h * 4 + 4, UW:YW], edgeE[:, ds(at + h * 4, 4), :]
                                  ).then_inc(L[1]["y"], 1)

            def merge(sn, back, b):
                def lk(n, ins):
                    ins.then_inc(L[1]["mg"], 1)
                    done(dve, 1, "mg", sn, back, n)
                mb = Mx[:, ds(b, 1), :]
                done(dve, 1, "U", sn, back)
                v.tensor_scalar(pen[:, :], ps[6][:, UW + H:YW], BIG, -BIG, ALU.mult, ALU.add)
                lk(1, v.tensor_tensor(nz[:, 0:1, :], ps[6][:, UW:UW + H].unsqueeze(1), adst[:, ds(b, 1), :],
                                      ALU.add))
                lk(2, v.scalar_tensor_tensor(nz[:, 1, :], nz[:, 0, :], 0.2, nz[:, 0, :], ALU.mult, ALU.max))
                lk(3, v.tensor_scalar(nz[:, 2, :], nz[:, 1, :], pen[:, 0:1], None, ALU.add))
                lk(4, v.tensor_tensor(mnew[:, :].unsqueeze(1), nz[:, 2:3, :], mb, ALU.max))
                v.tensor_tensor(dd[:, 0:1, :], mb, mnew[:, :].unsqueeze(1), ALU.subtract)
                lk(5, v.tensor_tensor(dd[:, 1, :], nz[:, 2, :], mnew[:, :], ALU.subtract))
                apart(dve)
                lk(6, v.tensor_copy(mb, mnew[:, :].unsqueeze(1)))
                done(dve, 1, "e", sn, back)
                ab = acc[:, ds(b, 1), :, :].rearrange("p b h d -> p (b h) d")
                lk(7, v.tensor_tensor(ab, ab, ee[:, 0, :].unsqueeze(2).to_broadcast([P, H, D + 1]), ALU.mult))
                done(dve, 1, "tm", sn, back)
                v.tensor_tensor(ab, ab, Tm[:, :, :], ALU.add).then_inc(L[1]["acc"], 1)
                done(dve, 1, "acc", sn, back)

            tiles = Past("tile", 1, 2 * TS - TG)
            blocks1 = Past("blk", 2, NB - 1)

            def steps1(i, q, half):
                maxima(i, q, half)
                dve.wait_ge(dst_in[half], (q + 1 + (NS - NS // 2 if half == 0 else NS // 2)) * 16)

                def step(sn, r, b):
                    at = tiles.back(1)
                    logits(sn, 1, at)
                    done(dve, 1, "sf", sn, 2)
                    onehot(1, sn, r, b, half, (sn % 2) * TG)
                    weigh(sn, 1, at)
                    merge(sn, 2, blocks1.back(2))
                    tiles.push(r * TG + half * TS)
                    blocks1.push(b)
                steps(dve, i, step)
                dve.sem_inc(free_d, 1)

            supers(dve, steps1)
            logits(STEPS, 1, tiles.back(1))
            weigh(STEPS, 1, tiles.back(1))
            merge(STEPS, 2, blocks1.back(2))
            merge(STEPS + 1, 2, blocks1.back(1))

            link(v.tensor_scalar(Mx[:, :, :], acc[:, :, :, D], 1e-16, None, ALU.add))
            link(v.reciprocal(Mx[:, :, :], Mx[:, :, :]))
            link(v.tensor_scalar(Mx[:, :, :], Mx[:, :, :], 1.0 / H, None, ALU.mult))
            link(v.memset(ones[:, :], 1.0))
            o2 = Y[:, 0:2, 0:H * D].rearrange("p t (h d) -> p t h d", h=H)
            with dve.Fori(0, NB // 2) as k:
                dve.wait_ge(fin["m"], k + 1)
                for t in range(2):
                    a = v.tensor_tensor(o2[:, t], acc[:, ds(k * 2 + t, 1), :, 0:D].rearrange("p b h d -> p (b h) d"),
                                        Mx[:, ds(k * 2 + t, 1), :].rearrange("p b h -> p (b h)").unsqueeze(2)
                                        .to_broadcast([P, H, D]), ALU.mult)
                a.then_inc(fin["st"], 1)
                dve.wait_ge(fin["m"], k + 2)
                v.tensor_tensor(x1[:, ds(k * 2, 2), 0:D], x1[:, ds(k * 2, 2), 0:D],
                                ps[6][:, 0:2 * D].rearrange("p (b d) -> p b d", b=2), ALU.add).then_inc(fin["v"], 1)
            dve.wait_ge(fin["v"], NB // 2 + 1)
            norm(1, lambda c: x1[:, ds(c * BC, BC), 0:D], lambda c: x1[:, ds(c * BC, BC), 0:D])

        @block.tensor
        def _(pe):
            t_ = nc.tensor
            pe.wait_ge(s["idn"], 2)
            for k in range(2):
                pe.wait_ge(s["rf"], k + 1)
                for c in range(NC):
                    n = P if c < NC - 1 else RL
                    u, j = k * NU + c // 4, c % 4
                    if j == 0 and u >= 2:
                        pe.wait_ge(s["rc"], u - 1)
                    last = t_.transpose(ps[u % 2][:, j * P:j * P + n], rows_f[0:n, c * P:c * P + P],
                                        ident[0:n, 0:n])
                    if j == 3 or c == NC - 1:
                        last.then_inc(s["rt"], 1)
            pe.wait_ge(s["load"], 16 * 16)
            with pe.Fori(0, NB // 2) as k:
                pe.wait_ge(tab0["st"], k + 1)
                for j in range(2):
                    last = t_.transpose(ps[4][0:D + 1, j * P:j * P + P], st2[:, j, :], ident[:, :])
                last.then_inc(tab0["tp"], 1)
                pe.wait_ge(tab0["tc"], k + 1)
                pe.wait_ge(tab0["v"], k + 1)
                for j in range(2):
                    last = t_.matmul(ps[5][:, j * 2 * D:(j + 1) * 2 * D], stT[:, j, :], w1[:, :],
                                     start=True, stop=True)
                last.then_inc(tab0["m"], 1)
            pe.wait_ge(s["bt"], 2)

            def transposes(l, sn, buf):
                m = L[l]
                for h in range(2):
                    done(pe, l, "S", sn, 0, h + 1)
                    o = ps[h][:, 0:2 * P].bitcast(bf16)
                    for t in range(4):
                        last = t_.transpose(o[:, t * P:t * P + P], S[:, ds(buf + (h * 4 + t), 1), :]
                                            .rearrange("p a n -> p (a n)"), identb[:, :])
                    last.then_inc(m["stp"], 1)

            def turn_h1(sn, back):
                for h in range(2):
                    done(pe, 0, "h", sn, back, h + 1)
                    for j in range(2):
                        last = t_.transpose(ps[2 + h][:, j * P:j * P + P],
                                            h1[:, h * 4 + 2 * j:h * 4 + 2 * j + 2, :].rearrange("p t d -> p (t d)"),
                                            ident[:, :])
                    last.then_inc(L[0]["htp"], 1)

            def first_product(sn, r, b, half):
                for h in range(2):
                    done(pe, 0, "sts", sn, 0, h + 1)
                    for k in range(3):
                        t_.matmul(ps[4 + h][:, 0:256], identb[:, :],
                                  g0[:, ds(r * TG + (half * TS + 4 * h), 4), k, :], start=(k == 0), stop=False,
                                  skip_group_check=True)
                    for t in range(4):
                        for k in range(3):
                            last = t_.matmul(ps[4 + h][:, t * D:t * D + D], ST[:, h * 4 + t, :],
                                             pq[:, ds(b, 1), k, 0:D], start=False, stop=(t == 3 and k == 2),
                                             skip_group_check=True)
                    last.then_inc(L[0]["z"], 1)

            def sums0(sn, back):
                done(pe, 0, "lo", sn, back)
                done(pe, 0, "acc", sn, back + 1)
                buf = ((sn + 2) % 4) * TG
                for t in range(TG):
                    for k in range(3):
                        last = t_.matmul(ps[6][:, 0:D], S[:, ds(buf + t, 1), :].rearrange("p a n -> p (a n)"),
                                         h2p[:, k, t * D:t * D + D], start=(t + k == 0),
                                         stop=(t == TG - 1 and k == 2))
                last.then_inc(L[0]["U"], 1)

            def second_product(sn, back):
                t_.matmul(ps[7][:, :], onesb[:, :], b2q[:, :], start=True, stop=False, skip_group_check=True)
                for j in range(4):
                    if j % 2 == 0:
                        done(pe, 0, "hts", sn, back, j // 2 + 1)
                    last = t_.matmul(ps[7][:, j * P:j * P + P], h1T[:, j, :], w2d[:, :], start=False,
                                     stop=(j == 3), skip_group_check=True)
                last.then_inc(L[0]["z2"], 1)

            def steps0(i, q, half):
                pe.wait_ge(gath[0][half], q * (16 * TS) + 16 * TS)
                pe.sem_inc(gdone, 1)
                def step(sn, r, b):
                    transposes(0, sn, (sn % 4) * TG)
                    turn_h1(sn, 1)
                    first_product(sn, r, b, half)
                    sums0(sn, 2)
                    second_product(sn, 1)
                steps(pe, i, step)

            pe.wait_ge(s["b2in"], 16)
            pe.wait_ge(s["idb"], 1)
            prime(pe, 0, "stp htp z U z2")
            pe.sem_inc(gdone, 2)
            pe.wait_ge(clean, 1)
            supers(pe, steps0)
            turn_h1(STEPS, 1)
            sums0(STEPS, 2)
            second_product(STEPS, 1)
            sums0(STEPS + 1, 2)

            with pe.Fori(0, NB // 2) as k:
                pe.wait_ge(tab1["st"], k + 1)
                apart(pe)
                for j in range(2):
                    last = t_.transpose(ps[4][0:D, j * P:j * P + P], st2[:, j, 0:D], ident[:, :])
                last.then_inc(tab1["tp"], 1)
                pe.wait_ge(tab1["tc"], k + 1)
                pe.wait_ge(tab1["v"], k * 2 + 1)
                for j in range(2):
                    last = t_.matmul(ps[5][:, j * 2 * H:(j + 1) * 2 * H], stT[0:D, j, :], va[:, :], start=True, stop=True)
                last.then_inc(tab1["m"], 1)

            def turns(i):
                pe.wait_ge(sgv, i * 4 + 2)
                apart(pe)
                for j in range(TG):
                    last = t_.transpose(ps[3 + j // 4][0:32, (j % 4) * P:(j % 4) * P + P], edgeA[:, j, :], ident[:, :])
                last.then_inc(sgp, 1)
                rowM = rowD[:, :].bitcast(f32)
                pe.wait_ge(sgv, i * 4 + 4)
                apart(pe)
                for j in range(TG):
                    t_.transpose(ps[5][:, j * 32:j * 32 + 32], rowM[:, j * P:(j + 1) * P], ident[0:32, 0:32])
                for j in range(TG):
                    last = t_.transpose(ps[5][:, 256 + j * GS:256 + j * GS + GS],
                                        rowF[0:GS, j * P:(j + 1) * P], ident[0:GS, 0:GS])
                last.then_inc(sgp, 1)

            def sums1(sn, back):
                for h in range(2):
                    if h == 0:
                        done(pe, 1, "acc", sn, back + 1)
                    done(pe, 1, "sf", sn, back, h + 1)
                    done(pe, 1, "y", sn, back, h + 1)
                    for t in range(h * 4, h * 4 + 4):
                        last = t_.matmul(ps[6][:, 0:YW], Sf[:, t, :], Y[:, t, :], start=(t == 0), stop=(t == 7))
                    last.then_inc(L[1]["U"], 1)

            def steps1(i, q, half):
                turns(i)
                def step(sn, r, b):
                    transposes(1, sn, (sn % 2) * TG)
                    done(pe, 1, "zc", sn, 1, 1)
                    for h in range(2):
                        done(pe, 1, "sts", sn, 0, h + 1)
                        for t in range(h * 4, h * 4 + 4):
                            last = t_.matmul(ps[2][:, t * 3 * H:(t + 1) * 3 * H], ST[:, t, :],
                                             adp[:, ds(b, 1), :, :].rearrange("p b k h -> p (b k h)"),
                                             start=True, stop=True)
                    last.then_inc(L[1]["ad"], 1)
                    sums1(sn, 1)
                steps(pe, i, step)

            prime(pe, 1, "stp ad U")
            pe.wait_ge(clean, 2)
            supers(pe, steps1)
            sums1(STEPS, 1)

            with pe.Fori(0, NB // 2) as k:
                pe.wait_ge(fin["st"], k + 1)
                for j in range(2):
                    for u in range(2):
                        last = t_.transpose(ps[4][:, (j * 2 + u) * P:(j * 2 + u + 1) * P],
                                            Y[:, j, u * P:u * P + P], ident[:, :])
                last.then_inc(fin["tp"], 1)
                pe.wait_ge(fin["tc"], k + 1)
                pe.wait_ge(fin["v"], k + 1)
                for j in range(2):
                    o = ps[6][:, j * D:j * D + D]
                    t_.matmul(o, Sf[:, j * 2, :], wf[:, 0, :], start=True, stop=False)
                    t_.matmul(o, Sf[:, j * 2 + 1, :], wf[:, 1, :], start=False, stop=False)
                    last = t_.matmul(o, ones[:, :], biasr[:, :], start=False, stop=True)
                last.then_inc(fin["m"], 1)

        @block.scalar
        def _(act):
            a_ = nc.scalar
            with nc.allow_non_contiguous_dma(reason="one destination per group"):
                act.dma_start(Bt[0:1, GS:GS + NG], dst.rearrange("(g e) -> g e", e=64)[0::GE // 64, 0:1]
                              .rearrange("g e -> e g")).then_inc(s["b_ld"], 16)
            for k, a in enumerate((src, dst)):
                if k:
                    act.wait_ge(s["rf"], 1)
                act.dma_start(rows_i[:, 0:(NC - 1) * P].rearrange("p (c e) -> p c e", e=P),
                              a[0:(NC - 1) * P * P].rearrange("(c p e) -> p c e", p=P, e=P)
                              ).then_inc(s["rows_in"], 16)
                act.dma_start(rows_i[0:RL, (NC - 1) * P:NC * P],
                              a[(NC - 1) * P * P:E].rearrange("(p e) -> p e", e=P)).then_inc(s["rows_in"], 16)
            for k, table in enumerate((srcT, dstT)):
                for q in range(NU):
                    act.wait_ge(s["rt"], k * NU + q + 1)
                    n = min(4 * P, NT - q * 4 * P)
                    a_.copy(table[:, q * 4 * P:q * 4 * P + n], ps[(k * NU + q) % 2][:, 0:n]).then_inc(s["rc"], 1)

            def copied(m, rows):
                with act.Fori(0, NB // 2) as k:
                    act.wait_ge(m["tp"], k + 1)
                    a_.copy(stT[0:rows, :, :], ps[4][0:rows, 0:2 * P].rearrange("p (a b) -> p a b", a=2)
                            ).then_inc(m["tc"], 1)

            copied(tab0, D + 1)
            act.wait_ge(s["bt"], 2)

            def to_sbuf(l, sn):
                for h in range(2):
                    done(act, l, "stp", sn, 0, h + 1)
                    a_.copy(ST[:, h * 4:h * 4 + 4, :],
                            ps[h][:, 0:2 * P].bitcast(bf16).rearrange("p (t n) -> p t n", t=4)
                            ).then_inc(L[l]["sts"], 1)

            def h1_out(sn, back):
                for h in range(2):
                    done(act, 0, "htp", sn, back, h + 1)
                    a_.copy(h1T[:, h * 2:h * 2 + 2, :], ps[2 + h][:, 0:2 * P].rearrange("p (t n) -> p t n", t=2)
                            ).then_inc(L[0]["hts"], 1)

            def parts(sn, back):
                m = L[0]
                done(act, 0, "z2", sn, back)
                a_.mul(az2, ps[7][:, :], 0.01).then_inc(m["az2"], 1)
                done(act, 0, "h2", sn, back)
                a_.copy(h2p[:, 0, :], h2).then_inc(m["hi"], 1)
                done(act, 0, "rest", sn, back)
                a_.copy(h2p[:, 1, :], h2).then_inc(m["mid"], 1)

            def steps0(i, q, half):
                def step(sn, r, b):
                    to_sbuf(0, sn)
                    h1_out(sn, 1)
                    for h in range(2):
                        done(act, 0, "z", sn, 0, h + 1)
                        a_.mul(az1[:, h * 4:h * 4 + 4, :],
                               ps[4 + h][:, 0:256].rearrange("p (t d) -> p t d", d=D), 0.01
                               ).then_inc(L[0]["az"], 1)
                    parts(sn, 1)
                steps(act, i, step)

            prime(act, 0, "sts hts az az2 hi mid")
            act.wait_ge(clean, 1)
            supers(act, steps0)
            h1_out(STEPS, 1)
            parts(STEPS, 1)

            def roots(base):
                with act.Fori(0, NCH) as c:
                    act.wait_ge(lna, c * 2 + (base * 2 * NCH + 1))
                    vv = var[:, ds(c * BC, BC)]
                    a_.activation(vv, vv, ACT.Sqrt).then_inc(lna, 1)

            roots(0)
            copied(tab1, D)

            def weights(sn, back):
                done(act, 1, "zc", sn, back)
                a_.activation(wb[:, :, :], dw[:, :, :], ACT.Exp).then_inc(L[1]["w"], 1)

            def factors(sn, back):
                done(act, 1, "mg", sn, back, 5)
                a_.activation(ee[:, :, :], dd[:, :, :], ACT.Exp).then_inc(L[1]["e"], 1)
                done(act, 1, "e", sn, back)
                for h in range(H):
                    a = a_.activation(Tm[:, h, :], ps[6][:, h * (D + 1):(h + 1) * (D + 1)], ACT.Copy,
                                      scale=ee[:, 1, h:h + 1])
                a.then_inc(L[1]["tm"], 1)

            def steps1(i, q, half):
                def step(sn, r, b):
                    to_sbuf(1, sn)
                    weights(sn, 1)
                    factors(sn, 2)
                    for h in range(2):
                        done(act, 1, "U", sn, 1, h + 1)
                        a_.copy(Sf[:, h * 4:h * 4 + 4, :], S[:, ds((sn % 2) * TG + 4 * h, 4), :]
                                ).then_inc(L[1]["sf"], 1)
                steps(act, i, step)

            prime(act, 1, "sts w sf e tm")
            act.wait_ge(clean, 2)
            supers(act, steps1)
            weights(STEPS, 1)
            factors(STEPS, 2)
            factors(STEPS + 1, 2)

            with act.Fori(0, NB // 2) as k:
                act.wait_ge(fin["tp"], k + 1)
                a_.copy(Sf[:, 0:4, :], ps[4][:, :].rearrange("p (t n) -> p t n", t=4)).then_inc(fin["tc"], 1)
            roots(1)


_IN = ["x", "src", "dst", "L0_gnn_W1", "L0_gnn_b1", "L0_gnn_W2", "L0_gnn_b2", "L1_gnn_W", "L1_gnn_att_src",
       "L1_gnn_att_dst", "L1_gnn_bias"]


def kernel(**inputs):
    import numpy as _np
    import concourse.bacc as _bacc
    from concourse import mybir as _mybir
    from concourse.bass_utils import run_bass_kernel_spmd as _run

    nc = _bacc.Bacc("TRN2", target_bir_lowering=False, num_devices=1)
    f32, i32 = _mybir.dt.float32, _mybir.dt.int32
    arrays, args = {}, []
    for name in _IN:
        a = _np.ascontiguousarray(inputs[name])
        arrays["in_" + name] = a
        args.append(nc.dram_tensor("in_" + name, a.shape, _mybir.dt.from_np(a.dtype), kind="ExternalInput").ap())
    args.append(nc.dram_tensor("out_0", (N, D), f32, kind="ExternalOutput").ap())
    for name, shape, dt in (("q_dram", (NB * P, BF), _mybir.dt.bfloat16), ("x_dram", (NB * P, XW), f32),
                            ("srcT_dram", (P, T), i32), ("dstT_dram", (P, T), f32), ("dst_dram", (EP,), i32)):
        args.append(nc.dram_tensor(name, shape, dt, kind="Internal").ap())
    build(nc, *args)
    r = _run(nc, [arrays], core_ids=[0])
    return r.results[0]["out_0"]
```

```python
import concourse.bass as bass
from concourse import mybir
from contextlib import ExitStack

N, E, D, H = 12500, 400000, 64, 4
P = 128
NB = -(-N // P)
LAST = N - (NB - 1) * P
TG = 8
GE = TG * P
GS = 8
TS = TG * GS
NT = E // P
NG = -(-E // GE)
NS = -(-NG // GS)
G = NS * GS
T = G * TG
EP = T * P
XW = D + 1 + H
UW = H * (D + 1)
YW = UW + H + 1
BIG = 2.0 ** 100
STEPS = G + NB - 1
PAST = GS + 3
BF = 3 * D
PADNODE = 1000000
NC = -(-NT // P)
RL = NT - (NC - 1) * P
NU = -(-NC // 4)
NCH = 7
BC = NB // NCH
LN_OPS = 7
EPS = 1e-5


def build(nc, x, src, dst, W1, b1, W2, b2, W, att_src, att_dst, bias, out, q_dram, x_dram, srcT_dram,
          dstT_dram, dst_dram):
    f32, i32, bf16 = mybir.dt.float32, mybir.dt.int32, mybir.dt.bfloat16
    ALU, ACT, AX = mybir.AluOpType, mybir.ActivationFunctionType, mybir.AxisListType
    ds = bass.ds
    ctx = ExitStack()
    with ctx:
        def sb(name, shape, dt=f32):
            return ctx.enter_context(nc.sbuf_tensor(name, shape, dt))

        def sem(name):
            return ctx.enter_context(nc.semaphore(name))

        state = sb("state", [P, NB * UW])
        big = sb("big", [P, 2 * TS * XW + NB * XW])
        x1 = big[:, 2 * TS * XW:].rearrange("p (b d) -> p b d", d=XW)
        S = sb("S", [P, 4 * TG, P], bf16)
        ST = sb("ST", [P, TG, P], bf16)
        Y = sb("Y", [P, TG, YW])
        rowD = sb("rowD", [32, GE], i32)
        rowX = sb("rowX", [P, GE + 1])
        rowR = rowX[0:32, :]
        rowA = sb("rowA", [P, GE])
        rowF = rowA[0:32, :]
        idx = sb("idx", [P, 2, TS], i32)
        dstc = sb("dstc", [P, 2, TS])
        edgeM = sb("edgeM", [P, 2 * TS, H])
        edgeE = sb("edgeE", [P, 2 * TS, H + 1])
        edgeA = sb("edgeA", [P, TG, 32])
        ident = sb("ident", [P, P])
        identb = sb("identb", [P, P], bf16)
        iotaf = rowX[:, 0:P]
        iota = sb("iota", [P, P], bf16)
        blk = sb("blk", [P, NB])
        Bt = sb("Bt", [1, GS + G + 1], i32)
        rel = sb("rel", [P, TG], bf16)
        adst = sb("adst", [P, NB, H])
        adp = sb("adp", [P, NB, 3, H], bf16)
        Mx = sb("Mx", [P, NB, H])
        adx = sb("adx", [P, TG, H])
        zz = sb("zz", [P, 2, TG, H])
        lz = sb("lz", [P, 2, TG, H])
        dw = sb("dw", [P, TG, H])
        wb = sb("wb", [P, TG, H])
        nz = sb("nz", [P, 3, H])
        mnew = sb("mnew", [P, H])
        warm = sb("warm", [P, 2])
        dd = sb("dd", [P, 2, H])
        ee = sb("ee", [P, 2, H])
        Tm = sb("Tm", [P, H, D + 1])
        ones = rowX[0:1, 0:P]
        wsb = rowA[0:D, 0:H * D]
        attb = rowA[0:D, H * D:3 * H * D].rearrange("p (a c) -> p a c", a=2)
        w1 = rowA[0:D + 1, 3 * H * D:3 * H * D + 2 * D]
        va = rowA[0:D, 3 * H * D + 2 * D:3 * H * D + 2 * D + 2 * H]
        mv = edgeA[:, :, :].rearrange("p j c -> p (j c)")
        mean, var = mv[:, 0:NB], mv[:, NB:2 * NB]
        max_flat = edgeM[:, :, :].rearrange("p t h -> p (t h)")
        edge_flat = edgeE[:, :, :].rearrange("p t h -> p (t h)")
        stT = max_flat[0:D + 1, 0:2 * P].rearrange("p (a b) -> p a b", a=2)
        b2q = max_flat[0:3, 2 * P:2 * P + TG * D // 2].bitcast(bf16)
        wf = max_flat[:, 0:2 * D].rearrange("p (a d) -> p a d", a=2)
        biasr = edge_flat[0:1, 0:D]
        st2 = edge_flat[:, 0:2 * D + 2].rearrange("p (b d) -> p b d", b=2)
        w2d = edge_flat[:, 2 * D + 2:4 * D + 2]
        onesb = edge_flat[0:3, 4 * D + 2:4 * D + 2 + P // 2].bitcast(bf16)
        Yf = Y[:, :, :].rearrange("p t d -> p (t d)")
        b2r = Yf[0:1, 0:2 * TG * D].rearrange("p (a c) -> p a c", a=2)
        b2p = Yf[0:1, 2 * TG * D:2 * TG * D + 3 * TG * D // 2].bitcast(bf16).rearrange("p (k c) -> p k c", k=3)

        pu = ctx.enter_context(nc.psum_tensor("pu", [P, 2 * 512], f32))
        ps = [ctx.enter_context(nc.psum_tensor(f"ps{i}", [P, 512], f32)) for i in range(6)]
        ps += [pu[:, 0:512], pu[:, 512:1024]]

        x0 = state[:, 0:NB * D].rearrange("p (b d) -> p b d", d=D)
        pq = state[:, NB * D:4 * NB * D].bitcast(bf16).rearrange("p (b k c) -> p b k c", k=3, c=2 * D)
        acc = state[:, :].rearrange("p (b h d) -> p b h d", h=H, d=D + 1)
        g0 = big[:, 0:TS * BF].bitcast(bf16).rearrange("p (t k d) -> p t k d", k=3, d=D)
        g0r = big[:, 0:TS * BF].bitcast(bf16).rearrange("p (t d) -> p t d", d=BF)
        g1 = big[:, 0:2 * TS * XW].rearrange("p (t d) -> p t d", d=XW)
        h1 = Yf[:, 0:TG * D].rearrange("p (t d) -> p t d", d=D)
        az1 = Yf[:, TG * D:2 * TG * D].rearrange("p (t d) -> p t d", d=D)
        az2 = Yf[:, 2 * TG * D:3 * TG * D]
        h2 = Yf[:, 3 * TG * D:4 * TG * D]
        h2p = rowX[:, 0:3 * TG * D // 2].bitcast(bf16).rearrange("p (k c) -> p k c", k=3)
        h1T = rowA[:, 0:4 * P].rearrange("p (t e) -> p t e", e=P)
        Sf = S[:, 2 * TG:4 * TG, :].rearrange("p t n -> p (t n)").bitcast(f32).rearrange("p (t n) -> p t n", n=P)
        rows_i = big[:, 0:NC * P].bitcast(i32)
        rows_f = big[:, NC * P:2 * NC * P]
        srcT = big[:, 2 * NC * P:2 * NC * P + T].bitcast(i32)
        dstT = big[:, 2 * NC * P + T:2 * NC * P + 2 * T]
        ln_t = big[:, 0:BC * D].rearrange("p (b d) -> p b d", d=D)
        res = rowX[:, 0:4 * D].rearrange("p (b c) -> p b c", b=2)

        names = "idb b2 b2in load clr wf pad cst idn b_ld bt rows_in rf rt rc q_out t_out d_out".split()
        s = {n: sem("s_" + n) for n in names}
        idx_in = [sem("idx_in0"), sem("idx_in1")]
        dst_in = [sem("dst_in0"), sem("dst_in1")]
        gath = [[sem(f"gath{l}{p}") for p in range(2)] for l in range(2)]
        row_in = sem("row_in")
        fredge_flatd = sem("fredge_flatd")
        gdone = sem("gdone")
        LAGS = [{"rel": 0, "S": 0, "stp0": 0, "stp1": 0, "sts0": 0, "sts1": 0, "z0": 0, "z1": 0, "az0": 0,
                 "az1": 0, "h0": 1, "h1": 1, "htp0": 1, "htp1": 1, "hts0": 1, "hts1": 1, "z2": 1, "az2": 1,
                 "h2": 2, "hi": 2, "rest": 2, "mid": 2, "lo": 3, "U": 3, "acc": 4},
                {"rel": 0, "S": 0, "stp0": 0, "stp1": 0, "sts0": 0, "sts1": 0, "ad": 0, "adx": 1, "zz": 1,
                 "lz": 1, "dw": 1, "w": 1, "sf0": 1, "sf1": 2, "y0": 2, "y1": 2, "U0": 2, "U1": 2, "nz": 3,
                 "nl": 3, "np": 3, "mnew": 3, "dd": 3, "e": 3, "mb": 3, "tm": 3, "old": 3, "acc": 4}]
        L = [{n: sem(f"l{l}_{n}") for n in LAGS[l]} for l in range(2)]

        class Turn:
            def __init__(self, eng, l, sn, r=0, b=0, tail=-1):
                self.eng, self.l, self.sn, self.r, self.b, self.tail = eng, l, sn, r, b, tail
                self.values = {}

            def has(self, lag):
                return lag > self.tail

            def after(self, stage, back):
                if back not in self.values:
                    value = self.sn + (PAST + 1 - back)
                    self.values[back] = value if isinstance(value, int) else self.eng.snap(value)
                self.eng.wait_ge(L[self.l][stage], self.values[back])

        class Past:
            def __init__(self, eng, name, n, top):
                self.eng, self.top = eng, top
                self.regs = [eng.alloc_register(f"{name}{j}") for j in range(n)]
                for x in self.regs:
                    eng.reg_mov(x, 0)

            def back(self, n):
                return self.eng.snap(self.regs[n - 1], min_val=0, max_val=self.top)

            def push(self, value):
                for a, b in zip(self.regs[::-1], self.regs[-2::-1]):
                    self.eng.reg_mov(a, b)
                self.eng.reg_mov(self.regs[0], value)

        def tails(eng, l, turn):
            for k in range(4):
                turn(Turn(eng, l, STEPS + k, tail=k))

        def prime(eng, l, names):
            for n in names.split():
                eng.sem_inc(L[l][n], PAST - LAGS[l][n])

        spl = sem("split")
        clean = sem("clean")
        dvs = sem("sg_chain")
        sgp, sgv = sem("sg_pe"), sem("sg_dve")
        lnv = sem("ln_dve")
        lna = sem("ln_act")
        vch = sem("dve_chain")
        tab0, tab1, fin = [{n: sem(f"{t}_{n}") for n in "st tp tc m v".split()}
                           for t in ("tab0", "tab1", "fin")]
        idle = sem("idle")
        x_out = sem("x_out")
        o_out = sem("o_out")

        block = ctx.enter_context(nc.Block())

        def supers(eng, body):
            with eng.Fori(0, NS // 2) as q:
                body(q * 2, q, 0)
                body(q * 2 + 1, q, 1)
            if NS % 2:
                body(NS - 1, NS // 2, 0)

        def apart(eng):
            eng.sem_inc(idle, 1)

        def steps(eng, l, i, first, turn):
            apart(eng)
            with eng.Fori(0, GS) as r:
                g = i * GS + r
                b0 = eng.snap(first, min_val=0, max_val=NB - 1)
                b1 = eng.value_load(Bt[0:1, ds(g + (GS + 1), 1)], min_val=0, max_val=NB - 1)
                with eng.Fori(b0, b1 + 1) as b:
                    turn(Turn(eng, l, eng.snap(g + b), r, b))
                eng.reg_mov(first, b1)

        def first_block(eng, name):
            first = eng.alloc_register(name)
            eng.reg_mov(first, eng.value_load(Bt[0:1, GS:GS + 1], min_val=0, max_val=NB - 1))
            return first

        @block.sync
        def _(sp):
            xr = x[0:(NB - 1) * P, :].rearrange("(b p) d -> p b d", p=P)
            sp.wait_ge(s["clr"], 1)
            sp.dma_start(x0[:, 0:NB - 1, :], xr).then_inc(s["load"], 16)
            sp.dma_start(x0[0:LAST, NB - 1, :], x[(NB - 1) * P:N, :]).then_inc(s["load"], 16)
            sp.dma_start(w1[0:D, 0:D], W1[0:D, :]).then_inc(s["load"], 16)
            sp.dma_start(w1[0:D, D:2 * D], W1[D:2 * D, :]).then_inc(s["load"], 16)
            sp.dma_start(w1[D:D + 1, 0:D], b1.rearrange("(a d) -> a d", a=1)).then_inc(s["load"], 16)
            for h in range(2):
                sp.dma_start(w2d[h * D:(h + 1) * D, h * D:(h + 1) * D], W2[:, :]).then_inc(s["load"], 16)
            sp.dma_start(b2r[:, 0, 0:D], b2.rearrange("(a d) -> a d", a=1)).then_inc(s["load"], 16)
            sp.dma_start(wsb[:, :], W[:, :]).then_inc(s["load"], 16)
            sp.dma_start(attb[:, 0, :], att_src.rearrange("a h d -> a (h d)").to_broadcast([D, H * D])
                         ).then_inc(s["load"], 16)
            sp.dma_start(attb[:, 1, :], att_dst.rearrange("a h d -> a (h d)").to_broadcast([D, H * D])
                         ).then_inc(s["load"], 16)
            sp.dma_start(dst_dram[0:E].rearrange("(a c) -> a c", a=16),
                         dst.rearrange("(a c) -> a c", a=16)).then_inc(s["d_out"], 16)
            sp.wait_ge(s["pad"], 1)
            sp.dma_start(dst_dram[E:EP].rearrange("(a c) -> a c", a=2),
                         rowD[0:2, 0:(EP - E) // 2]).then_inc(s["d_out"], 16)
            sp.wait_ge(s["rc"], NU)
            sp.dma_start(srcT_dram[:, :], srcT).then_inc(s["t_out"], 16)
            sp.wait_ge(s["rc"], 2 * NU)
            sp.dma_start(dstT_dram[:, :], dstT).then_inc(s["t_out"], 16)
            sp.wait_ge(s["b2"], 1)
            sp.dma_start(b2q[:, :], b2p[0:1, :, :]).then_inc(s["b2in"], 16)
            sp.wait_ge(tab0["v"], NB // 2 + 1)
            for k in range(3):
                sp.dma_start(q_dram.rearrange("(b p) d -> p b d", p=P)[:, :, k * D:(k + 1) * D],
                             pq[:, :, k, D:2 * D]).then_inc(s["q_out"], 16)
            sp.wait_ge(s["t_out"], 32)

            for l in range(2):
                def chunk(i, q, half):
                    sp.wait_ge(gdone, i + (l * NS + 1))
                    sp.dma_start(idx[:, half, :], srcT_dram[:, ds(i * TS, TS)]).then_inc(idx_in[half], 16)
                    sp.wait_ge(fredge_flatd, i + (l * NS + 1))
                    sp.dma_start(dstc[:, half, :], dstT_dram[:, ds(i * TS, TS)]).then_inc(dst_in[half], 16)
                    if l:
                        sp.wait_ge(sgv, i * 4 + 1)
                        for h in range(H):
                            sp.dma_start(rowD[h * GS:(h + 1) * GS, :],
                                         dst_dram[ds(i * (GS * GE), GS * GE)].rearrange("(g e) -> g e", g=GS)
                                         ).then_inc(row_in, 16)
                if l:
                    sp.wait_ge(s["d_out"], 32)
                supers(sp, chunk)
                if l == 0:
                    sp.wait_ge(tab1["v"], 2 * (NB // 2) + 1)
                    sp.dma_start(x_dram.rearrange("(b p) d -> p b d", p=P), x1).then_inc(x_out, 16)
            sp.wait_ge(L[1]["acc"], STEPS + PAST)
            for h in range(H):
                sp.dma_start(wf[(h % 2) * D:(h % 2 + 1) * D, h // 2, :], W[:, h * D:(h + 1) * D]
                             ).then_inc(s["wf"], 16)
            sp.dma_start(biasr[:, :], bias.rearrange("(a d) -> a d", a=1)).then_inc(s["wf"], 16)
            sp.wait_ge(lnv, 2 * NCH * LN_OPS)
            sp.dma_start(out[0:(NB - 1) * P, :].rearrange("(b p) d -> p b d", p=P),
                         x1[:, 0:NB - 1, 0:D]).then_inc(o_out, 16)
            sp.dma_start(out[(NB - 1) * P:N, :], x1[0:LAST, NB - 1, 0:D]).then_inc(o_out, 16)
            sp.wait_ge(o_out, 32)

        @block.gpsimd
        def _(pool):
            nc.gpsimd.iota(iotaf[:, :], [[1, P]], base=0, channel_multiplier=0,
                           allow_small_or_imprecise_dtypes=True).then_inc(s["cst"], 1)
            nc.gpsimd.iota(blk[:, :], [[P, NB]], base=0, channel_multiplier=0,
                           allow_small_or_imprecise_dtypes=True).then_inc(s["cst"], 1)
            nc.gpsimd.memset(ident[:, :], 0.0).then_inc(s["idn"], 1)
            pool.wait_ge(s["idn"], 1)
            nc.gpsimd.affine_select(out=ident[:, :], in_=ident[:, :], compare_op=ALU.not_equal, fill=1.0,
                                    base=0, pattern=[[-1, P]], channel_multiplier=1).then_inc(s["idn"], 1)
            for l in range(2):
                if l == 0:
                    pool.wait_ge(s["q_out"], 48)
                    pool.wait_ge(s["bt"], 2)
                    pool.wait_ge(s["t_out"], 32)
                else:
                    pool.wait_ge(x_out, 16)

                def gathers(i, q, half):
                    n = q + 1 + (0 if l == 0 else (NS - NS // 2 if half == 0 else NS // 2))
                    pool.wait_ge(idx_in[half], n * 16)
                    gone = pool.value_load(Bt[0:1, ds(i * GS, 1)], min_val=0, max_val=NB - 1)
                    pool.wait_ge(L[l]["y1" if l else "z1"], i * GS + gone + (PAST - GS))
                    apart(pool)
                    for t in range(TS):
                        o = (g1 if l else g0r)[:, half * TS + t, :]
                        nc.gpsimd.indirect_dma_start(
                            o, None, x_dram if l else q_dram,
                            bass.IndirectOffsetOnAxis(ap=idx[:, half, t:t + 1], axis=0)
                        ).then_inc(gath[l][half], 16)
                supers(pool, gathers)

        @block.vector
        def _(dve):
            v = nc.vector
            count = [0]

            def link(ins):
                count[0] += 1
                ins.then_inc(vch, 1)
                dve.wait_ge(vch, count[0])

            link(v.memset(x0[:, NB - 1, :], 0.0))
            link(v.memset(onesb[:, :], 1.0))
            link(v.memset(w2d[:, :], 0.0))
            v.memset(w1[D:D + 1, D:2 * D], 0.0).then_inc(s["clr"], 1)
            v.memset(rowD[:, :], PADNODE).then_inc(s["pad"], 1)
            link(v.memset(st2[:, :, D:D + 1], 1.0))
            link(v.memset(S[:, :, :], 0.0))
            for t in (tab0, tab1, fin):
                dve.sem_inc(t["v"], 1)
            dve.sem_inc(sgv, 1)
            link(v.memset(srcT[:, NT:T], 0))
            link(v.memset(dstT[:, NT:T], float(PADNODE)))
            dve.wait_ge(s["b_ld"], 16)
            v.memset(Bt[0:1, 0:GS], 0).then_inc(s["bt"], 1)
            link(v.tensor_scalar(Bt[0:1, GS:GS + NG], Bt[0:1, GS:GS + NG], 7, None, ALU.arith_shift_right))
            v.memset(Bt[0:1, GS + NG:GS + G + 1], NB - 1).then_inc(s["bt"], 1)
            for k in range(2):
                dve.wait_ge(s["rows_in"], 32 * (k + 1))
                if k:
                    dve.wait_ge(s["rt"], NU)
                link(v.tensor_copy(rows_f[:, 0:(NC - 1) * P], rows_i[:, 0:(NC - 1) * P]))
                v.tensor_copy(rows_f[0:RL, (NC - 1) * P:NC * P],
                              rows_i[0:RL, (NC - 1) * P:NC * P]).then_inc(s["rf"], 1)
            dve.wait_ge(s["load"], 11 * 16)
            link(v.tensor_tensor(w1[0:D, 0:D], w1[0:D, 0:D], w1[0:D, D:2 * D], ALU.subtract))
            for k in range(2):
                link(v.tensor_tensor(attb[:, k, :], attb[:, k, :], wsb[:, :], ALU.mult))
                link(v.tensor_reduce(va[:, k * H:(k + 1) * H],
                                     attb[:, k, :].rearrange("p (h d) -> p h d", h=H), AX.X, ALU.add))
            link(v.tensor_copy(b2r[:, 1, :].rearrange("p (t d) -> p t d", d=D),
                               b2r[:, 0:1, 0:D].to_broadcast([1, TG, D])))
            link(v.tensor_copy(b2p[:, 0, :], b2r[:, 1, :]))
            link(v.tensor_tensor(b2r[:, 1, :], b2r[:, 1, :], b2p[:, 0, :], ALU.subtract))
            link(v.tensor_copy(b2p[:, 1, :], b2r[:, 1, :]))
            v.tensor_tensor(b2p[:, 2, :], b2r[:, 1, :], b2p[:, 1, :], ALU.subtract).then_inc(s["b2"], 1)
            def passes(t, give, receive):
                give(0)
                with dve.Fori(0, NB // 2 - 1) as k:
                    dve.wait_ge(t["tp"], k + 1)
                    give(k + 1)
                    dve.wait_ge(t["m"], k + 1)
                    receive(k)
                dve.wait_ge(t["m"], NB // 2)
                receive(NB // 2 - 1)

            dve.wait_ge(s["cst"], 2)
            dve.wait_ge(s["idn"], 2)
            link(v.tensor_copy(iota[:, :], iotaf[:, :]))
            v.tensor_copy(identb[:, :], ident[:, :]).then_inc(s["idb"], 1)
            def give0(k):
                v.tensor_copy(st2[:, :, 0:D], x0[:, ds(k * 2, 2), :]).then_inc(tab0["st"], 1)

            def receive0(k):
                pv = ps[5][:, 0:4 * D].rearrange("p (b c) -> p b c", b=2)

                def part(n):
                    return pq[:, ds(k * 2, 2), n, :]

                def split(n, ins):
                    ins.then_inc(spl, 1)
                    dve.wait_ge(spl, k * 3 + n)
                split(1, v.tensor_copy(part(0), pv))
                split(2, v.tensor_tensor(res, pv, part(0), ALU.subtract))
                split(3, v.tensor_copy(part(1), res))
                v.tensor_tensor(part(2), res, part(1), ALU.subtract).then_inc(tab0["v"], 1)

            passes(tab0, give0, receive0)

            def hv(ap, h):
                return ap[:, h * 4:(h + 1) * 4, :]

            def onehot(k, half, buf):
                k.after("S", 1)
                v.tensor_scalar(rel[:, :], dstc[:, half, ds(k.r * TG, TG)], blk[:, ds(k.b, 1)], None,
                                ALU.subtract).then_inc(L[k.l]["rel"], 1)
                k.after("rel", 0)
                v.tensor_tensor(S[:, ds(buf, TG), :], iota[:, :].unsqueeze(1).to_broadcast([P, TG, P]),
                                rel[:, :].unsqueeze(2).to_broadcast([P, TG, P]),
                                ALU.is_equal).then_inc(L[k.l]["S"], 1)

            blocks = Past(dve, "block", 4, NB - 1)

            def turn0(half):
                m = L[0]

                def turn(k):
                    if k.has(4):
                        b = blocks.back(4 - max(k.tail, 0))
                        k.after("U", 4)
                        k.after("acc", 5)
                        v.tensor_tensor(x0[:, ds(b, 1), :], x0[:, ds(b, 1), :],
                                        ps[6][:, 0:D].unsqueeze(1), ALU.add).then_inc(m["acc"], 1)
                    if k.has(3):
                        k.after("mid", 3)
                        v.tensor_tensor(h2p[:, 2, :], h2, h2p[:, 1, :], ALU.subtract).then_inc(m["lo"], 1)
                    if k.has(0):
                        onehot(k, half, (k.sn % 4) * TG)
                    elif k.has(3):
                        k.after("lo", 3)
                    if k.has(1):
                        for h in range(2):
                            k.after(f"az{h}", 1)
                            v.tensor_tensor(hv(h1, h), ps[4 + h][:, 0:256].rearrange("p (t d) -> p t d", d=D),
                                            hv(az1, h), ALU.max).then_inc(m[f"h{h}"], 1)
                    if k.has(2):
                        k.after("az2", 2)
                        v.tensor_tensor(h2, ps[7][:, :], az2, ALU.max).then_inc(m["h2"], 1)
                        k.after("hi", 2)
                        v.tensor_tensor(h2, h2, h2p[:, 0, :], ALU.subtract).then_inc(m["rest"], 1)
                    if k.has(0):
                        blocks.push(k.b)
                return turn

            first0 = first_block(dve, "first0")

            def steps0(i, q, half):
                dve.wait_ge(dst_in[half], (q + 1) * 16)
                steps(dve, 0, i, first0, turn0(half))
                dve.sem_inc(fredge_flatd, 1)

            prime(dve, 0, "rel S h0 h1 h2 rest lo acc")
            dve.sem_inc(fredge_flatd, 2)
            for n in (2, 3, 4, 5, 6, 7):
                link(v.memset(ps[n][:, :], 0.0))
            link(v.memset(rowX[:, :], 0.0))
            dve.wait_ge(s["b2in"], 16)
            link(v.memset(Y[:, :, :], 0.0))
            dve.sem_inc(clean, 1)
            supers(dve, steps0)
            tails(dve, 0, turn0(0))
            dve.wait_ge(L[0]["acc"], STEPS + PAST)
            link(v.memset(x1[:, :, D:D + 1], 1.0))

            def norm(first, y, o):
                base = first
                with dve.Fori(0, NCH) as c:
                    yy = y(c)
                    mm = mean[:, ds(c * BC, BC)]
                    vv = var[:, ds(c * BC, BC)]
                    k = [0]

                    def lk(ins):
                        k[0] += 1
                        ins.then_inc(lnv, 1)
                        dve.wait_ge(lnv, c * LN_OPS + (base * NCH * LN_OPS + k[0]))
                    lk(v.tensor_reduce(mm, yy, AX.X, ALU.add))
                    lk(v.tensor_scalar(mm, mm, 1.0 / D, None, ALU.mult))
                    lk(v.tensor_tensor(yy, yy, mm.unsqueeze(2).to_broadcast([P, BC, D]), ALU.subtract))
                    lk(v.tensor_tensor(ln_t, yy, yy, ALU.mult))
                    lk(v.tensor_reduce(vv, ln_t, AX.X, ALU.add))
                    v.tensor_scalar(vv, vv, 1.0 / D, EPS, ALU.mult, ALU.add).then_inc(lna, 1)
                    dve.wait_ge(lna, c * 2 + (base * 2 * NCH + 2))
                    apart(dve)
                    lk(v.reciprocal(vv, vv))
                    lk(v.tensor_tensor(o(c), yy, vv.unsqueeze(2).to_broadcast([P, BC, D]), ALU.mult))

            norm(0, lambda c: x0[:, ds(c * BC, BC), :], lambda c: x1[:, ds(c * BC, BC), 0:D])

            def give1(k):
                v.tensor_copy(st2[:, :, 0:D], x1[:, ds(k * 2, 2), 0:D]).then_inc(tab1["st"], 1)

            def receive1(k):
                pv = ps[5][:, 0:4 * H].rearrange("p (b c) -> p b c", b=2)
                v.tensor_copy(x1[:, ds(k * 2, 2), D + 1:XW], pv[:, :, 0:H]).then_inc(tab1["v"], 1)
                v.tensor_copy(adst[:, ds(k * 2, 2), :], pv[:, :, H:2 * H]).then_inc(tab1["v"], 1)

            passes(tab1, give1, receive1)
            dve.wait_ge(tab1["v"], 2 * (NB // 2) + 1)
            link(v.tensor_copy(adp[:, :, 0, :], adst[:, :, :]))
            link(v.tensor_tensor(Mx[:, :, :], adst[:, :, :], adp[:, :, 0, :], ALU.subtract))
            link(v.tensor_copy(adp[:, :, 1, :], Mx[:, :, :]))
            link(v.tensor_tensor(adp[:, :, 2, :], Mx[:, :, :], adp[:, :, 1, :], ALU.subtract))
            link(v.tensor_tensor(Mx[:, :, :], x1[:, :, D + 1:XW], adst[:, :, :], ALU.add))
            link(v.scalar_tensor_tensor(Mx[:, :, :], Mx[:, :, :], 0.2, Mx[:, :, :], ALU.mult, ALU.max))
            for h in range(H):
                link(v.tensor_copy(acc[:, :, h, :], x1[:, :, 0:D + 1]))
            link(v.memset(S[:, :, :], 0.0))
            link(v.memset(rowR[:, 0:1], -BIG))
            link(v.memset(rowR[:, GE:GE + 1], -BIG))
            link(v.memset(ps[2][:, :], 0.0))
            link(v.memset(ps[6][:, :], 0.0))
            link(v.memset(ps[7][:, :], 0.0))
            link(v.memset(Y[:, :, :], 0.0))
            link(v.memset(mnew[:, :], 0.0))
            link(v.memset(warm[:, :], 0.0))
            link(v.memset(wb[:, :, :], 0.0))
            link(v.memset(Tm[:, :, :], 0.0))
            prime(dve, 1, "rel S adx zz lz dw y0 y1 nz nl np mnew dd old acc")
            dve.sem_inc(clean, 1)

            def maxima(i, q, half):
                def lk(n, ins):
                    ins.then_inc(dvs, 1)
                    dve.wait_ge(dvs, i * 8 + n)
                dve.wait_ge(gath[1][half], q * (16 * TS) + 16 * TS)
                dve.sem_inc(gdone, 1)
                gt = g1[:, half * TS:(half + 1) * TS, D + 1:XW].rearrange("p (g j) h -> p j h g", j=TG)
                for h in range(H):
                    a = v.tensor_copy(edgeA[:, :, h * GS:(h + 1) * GS], gt[:, :, h, :])
                a.then_inc(sgv, 1)
                dve.wait_ge(row_in, i * (16 * H) + 16 * H)
                lk(1, v.tensor_tensor(rowR[:, 1:GE], rowD[:, 1:GE], rowD[:, 0:GE - 1], ALU.not_equal))
                lk(2, v.tensor_scalar(rowR[:, 1:GE], rowR[:, 1:GE], -BIG, None, ALU.mult))
                dve.wait_ge(sgp, i * 2 + 1)
                for h in range(2):
                    lk(3 + h, v.tensor_tensor_scan(rowF[:, h * 512:h * 512 + 512],
                                                   rowR[:, h * 512:h * 512 + 512], ps[3 + h][0:32, :],
                                                   -BIG if h == 0 else rowF[:, 511:512], ALU.add, ALU.max))
                rowM = rowD[:, :].bitcast(f32)
                v.tensor_tensor_scan(rowM[:, ::-1], rowR[:, 1:GE + 1][:, ::-1], rowF[:, ::-1],
                                     -BIG, ALU.add, ALU.max).then_inc(sgv, 1)
                dve.wait_ge(sgv, i * 4 + 3)
                v.tensor_scalar(rowF[0:GS, :], rowR[0:GS, 1:GE + 1], -1.0, None, ALU.is_lt).then_inc(sgv, 1)
                dve.wait_ge(sgp, i * 2 + 2)
                own = ds(half * TS, TS)
                pm = ps[5][:, 0:TG * 32].rearrange("p (j h g) -> p j h g", j=TG, h=H)
                for h in range(H):
                    a = v.tensor_copy(edgeM[:, own, h].rearrange("p (g j) -> p j g", j=TG), pm[:, :, h, :])
                lk(5, a)
                fl = ps[5][:, 256:256 + TG * GS].rearrange("p (j g) -> p j g", j=TG)
                lk(6, v.tensor_copy(edgeE[:, own, H].rearrange("p (g j) -> p j g", j=TG), fl))
                lk(7, v.tensor_tensor(edgeE[:, own, 0:H], edgeM[:, own, :],
                                      edgeE[:, own, H:H + 1].to_broadcast([P, TS, H]), ALU.mult))
                lk(8, v.tensor_scalar(edgeE[:, own, H].rearrange("p (g j) -> p j g", j=TG), fl, BIG, None,
                                      ALU.mult))
                dve.sem_inc(sgv, 1)

            tiles = Past(dve, "tile", 2, 2 * TS - TG)
            blocks1 = Past(dve, "blk", 4, NB - 1)

            def weigh(k, h, at):
                k.after(f"U{h}", 3)
                rows = slice(h * 4, h * 4 + 4)
                v.tensor_tensor(Y[:, rows, 0:UW].rearrange("p t (h d) -> p t h d", h=H),
                                g1[:, ds(at + h * 4, 4), 0:D + 1].unsqueeze(2).to_broadcast([P, 4, H, D + 1]),
                                wb[:, rows, :].unsqueeze(3).to_broadcast([P, 4, H, D + 1]),
                                ALU.mult).then_inc(L[1][f"y{h}"], 1)

            def turn1(half):
                m = L[1]

                def turn(k):
                    t = max(k.tail, 0)
                    if k.has(2):
                        at = tiles.back(2 - t)
                        k.after("w", 2)
                        weigh(k, 0, at)
                    if k.has(4):
                        ab = acc[:, ds(blocks1.back(4 - t), 1), :, :].rearrange("p b h d -> p (b h) d")
                        k.after("old", 4)
                        k.after("tm", 4)
                        v.tensor_tensor(ab, ab, Tm[:, :, :], ALU.add).then_inc(m["acc"], 1)

                    if k.has(1):
                        here = tiles.back(1)
                        zf = zz[:, :, :, :].rearrange("p a t h -> p (a t h)")
                        k.after("ad", 1)
                        v.tensor_reduce(adx[:, :, :],
                                        ps[2][:, 0:TG * 3 * H].rearrange("p (t k h) -> p t h k", k=3, h=H),
                                        AX.X, ALU.add).then_inc(m["adx"], 1)
                    if k.has(3):
                        b = blocks1.back(3 - t)
                        mb = Mx[:, ds(b, 1), :]
                        ends = pu[:, ds(((k.sn + 1) % 2) * 512, YW)]
                        k.after("U1", 3)
                        v.tensor_tensor(nz[:, 0:1, :], ends[:, UW:UW + H].unsqueeze(1), adst[:, ds(b, 1), :],
                                        ALU.add).then_inc(m["nz"], 1)
                    if k.has(1):
                        k.after("adx", 1)
                        v.tensor_tensor(zz[:, 0], g1[:, ds(here, TG), D + 1:XW], adx[:, :, :], ALU.add)
                        v.tensor_tensor(zz[:, 1], edgeM[:, ds(here, TG), :], adx[:, :, :], ALU.add
                                        ).then_inc(m["zz"], 1)
                    if k.has(3):
                        k.after("nz", 3)
                        v.scalar_tensor_tensor(nz[:, 1, :], nz[:, 0, :], 0.2, nz[:, 0, :], ALU.mult, ALU.max
                                               ).then_inc(m["nl"], 1)
                    if k.has(1):
                        k.after("zz", 1)
                        v.scalar_tensor_tensor(lz[:, :, :, :].rearrange("p a t h -> p (a t h)"), zf, 0.2, zf,
                                               ALU.mult, ALU.max).then_inc(m["lz"], 1)
                    if k.has(3):
                        k.after("nl", 3)
                        v.scalar_tensor_tensor(nz[:, 2, :], ends[:, UW + H:YW].to_broadcast([P, H]), -BIG,
                                               nz[:, 1, :], ALU.add, ALU.add).then_inc(m["np"], 1)
                    if k.has(1):
                        k.after("lz", 1)
                        v.tensor_tensor(dw[:, :, :], lz[:, 0], lz[:, 1], ALU.subtract).then_inc(m["dw"], 1)
                    if k.has(3):
                        k.after("np", 3)
                        v.tensor_tensor(mnew[:, :].unsqueeze(1), nz[:, 2:3, :], mb, ALU.max
                                        ).then_inc(m["mnew"], 1)
                        k.after("mnew", 3)
                        v.tensor_tensor(dd[:, 0:1, :], mb, mnew[:, :].unsqueeze(1), ALU.subtract)
                        v.tensor_tensor(dd[:, 1, :], nz[:, 2, :], mnew[:, :], ALU.subtract).then_inc(m["dd"], 1)

                    if k.has(0):
                        k.after("sf1", 2)
                        onehot(k, half, (k.sn % 2) * TG)
                    if k.has(2):
                        weigh(k, 1, at)
                    if k.has(3):
                        ab = acc[:, ds(b, 1), :, :].rearrange("p b h d -> p (b h) d")
                        k.after("e", 3)
                        v.tensor_tensor(ab, ab, ee[:, 0, :].unsqueeze(2).to_broadcast([P, H, D + 1]), ALU.mult
                                        ).then_inc(m["old"], 1)
                    if k.has(0):
                        tiles.push(k.r * TG + half * TS)
                        blocks1.push(k.b)
                return turn

            first1 = first_block(dve, "first1")

            def steps1(i, q, half):
                maxima(i, q, half)
                dve.wait_ge(dst_in[half], (q + 1 + (NS - NS // 2 if half == 0 else NS // 2)) * 16)
                steps(dve, 1, i, first1, turn1(half))
                dve.sem_inc(fredge_flatd, 1)

            supers(dve, steps1)
            tails(dve, 1, turn1(0))
            dve.wait_ge(L[1]["acc"], STEPS + PAST)

            link(v.tensor_scalar(Mx[:, :, :], acc[:, :, :, D], 1e-16, None, ALU.add))
            link(v.reciprocal(Mx[:, :, :], Mx[:, :, :]))
            link(v.tensor_scalar(Mx[:, :, :], Mx[:, :, :], 1.0 / H, None, ALU.mult))
            link(v.memset(ones[:, :], 1.0))
            o2 = Y[:, 0:2, 0:H * D].rearrange("p t (h d) -> p t h d", h=H)

            def give2(k):
                for t in range(2):
                    a = v.tensor_tensor(o2[:, t], acc[:, ds(k * 2 + t, 1), :, 0:D].rearrange("p b h d -> p (b h) d"),
                                        Mx[:, ds(k * 2 + t, 1), :].rearrange("p b h -> p (b h)").unsqueeze(2)
                                        .to_broadcast([P, H, D]), ALU.mult)
                a.then_inc(fin["st"], 1)

            def receive2(k):
                v.tensor_tensor(x1[:, ds(k * 2, 2), 0:D], x1[:, ds(k * 2, 2), 0:D],
                                ps[6][:, 0:2 * D].rearrange("p (b d) -> p b d", b=2), ALU.add).then_inc(fin["v"], 1)

            passes(fin, give2, receive2)
            dve.wait_ge(fin["v"], NB // 2 + 1)
            norm(1, lambda c: x1[:, ds(c * BC, BC), 0:D], lambda c: x1[:, ds(c * BC, BC), 0:D])

        @block.tensor
        def _(pe):
            t_ = nc.tensor
            pe.wait_ge(s["idn"], 2)
            for k in range(2):
                pe.wait_ge(s["rf"], k + 1)
                for c in range(NC):
                    n = P if c < NC - 1 else RL
                    u, j = k * NU + c // 4, c % 4
                    if j == 0 and u >= 2:
                        pe.wait_ge(s["rc"], u - 1)
                    last = t_.transpose(ps[u % 2][:, j * P:j * P + n], rows_f[0:n, c * P:c * P + P],
                                        ident[0:n, 0:n])
                    if j == 3 or c == NC - 1:
                        last.then_inc(s["rt"], 1)
            pe.wait_ge(s["load"], 11 * 16)
            with pe.Fori(0, NB // 2) as k:
                pe.wait_ge(tab0["st"], k + 1)
                for j in range(2):
                    last = t_.transpose(ps[4][0:D + 1, j * P:j * P + P], st2[:, j, :], ident[:, :])
                last.then_inc(tab0["tp"], 1)
                pe.wait_ge(tab0["tc"], k + 1)
                pe.wait_ge(tab0["v"], k + 1)
                for j in range(2):
                    last = t_.matmul(ps[5][:, j * 2 * D:(j + 1) * 2 * D], stT[:, j, :], w1[:, :],
                                     start=True, stop=True)
                last.then_inc(tab0["m"], 1)
            pe.wait_ge(s["bt"], 2)

            def transposes(k, buf):
                k.after("S", 0)
                hot = S[:, ds(buf, TG), :]
                for h in range(2):
                    k.after(f"sts{h}", 1)
                    o = ps[h][:, 0:2 * P].bitcast(bf16)
                    for t in range(4):
                        last = t_.transpose(o[:, t * P:t * P + P], hot[:, h * 4 + t, :], identb[:, :])
                    last.then_inc(L[k.l][f"stp{h}"], 1)

            def turn0(half):
                m = L[0]

                def turn(k):
                    if k.has(3):
                        buf = ((k.sn + 1) % 4) * TG
                        hot = S[:, ds(buf, TG), :]
                        k.after("lo", 3)
                        for t in range(TG):
                            for j in range(3):
                                last = t_.matmul(ps[6][:, 0:D],
                                                 hot[:, t, :],
                                                 h2p[:, j, t * D:t * D + D], start=(t + j == 0),
                                                 stop=(t == TG - 1 and j == 2))
                        last.then_inc(m["U"], 1)
                    if k.has(0):
                        transposes(k, (k.sn % 4) * TG)
                    if k.has(1):
                        for h in range(2):
                            k.after(f"h{h}", 1)
                            k.after(f"hts{h}", 2)
                            for j in range(2):
                                last = t_.transpose(ps[2 + h][:, j * P:j * P + P],
                                                    h1[:, h * 4 + 2 * j:h * 4 + 2 * j + 2, :]
                                                    .rearrange("p t d -> p (t d)"), ident[:, :])
                            last.then_inc(m[f"htp{h}"], 1)
                    if k.has(0):
                        for h in range(2):
                            k.after(f"sts{h}", 0)
                            for j in range(3):
                                t_.matmul(ps[4 + h][:, 0:256], identb[:, :],
                                          g0[:, ds(k.r * TG + (half * TS + 4 * h), 4), j, :], start=(j == 0),
                                          stop=False, skip_group_check=True)
                            for t in range(4):
                                for j in range(3):
                                    last = t_.matmul(ps[4 + h][:, t * D:t * D + D], ST[:, h * 4 + t, :],
                                                     pq[:, ds(k.b, 1), j, 0:D], start=False,
                                                     stop=(t == 3 and j == 2), skip_group_check=True)
                            last.then_inc(m[f"z{h}"], 1)
                    if k.has(1):
                        k.after("h2", 2)
                        t_.matmul(ps[7][:, :], onesb[:, :], b2q[:, :], start=True, stop=False,
                                  skip_group_check=True)
                        for j in range(4):
                            if j % 2 == 0:
                                k.after(f"hts{j // 2}", 1)
                            last = t_.matmul(ps[7][:, j * P:j * P + P], h1T[:, j, :], w2d[:, :], start=False,
                                             stop=(j == 3), skip_group_check=True)
                        last.then_inc(m["z2"], 1)
                return turn

            first0 = first_block(pe, "pe_first0")

            def steps0(i, q, half):
                pe.wait_ge(gath[0][half], q * (16 * TS) + 16 * TS)
                pe.sem_inc(gdone, 1)
                steps(pe, 0, i, first0, turn0(half))

            pe.wait_ge(s["b2in"], 16)
            pe.wait_ge(s["idb"], 1)
            prime(pe, 0, "stp0 stp1 htp0 htp1 z0 z1 U z2")
            pe.sem_inc(gdone, 2)
            pe.wait_ge(clean, 1)
            supers(pe, steps0)
            tails(pe, 0, turn0(0))

            with pe.Fori(0, NB // 2) as k:
                pe.wait_ge(tab1["st"], k + 1)
                apart(pe)
                for j in range(2):
                    last = t_.transpose(ps[4][0:D, j * P:j * P + P], st2[:, j, 0:D], ident[:, :])
                last.then_inc(tab1["tp"], 1)
                pe.wait_ge(tab1["tc"], k + 1)
                pe.wait_ge(tab1["v"], k * 2 + 1)
                for j in range(2):
                    last = t_.matmul(ps[5][:, j * 2 * H:(j + 1) * 2 * H], stT[0:D, j, :], va[:, :], start=True, stop=True)
                last.then_inc(tab1["m"], 1)

            def turns(i):
                pe.wait_ge(sgv, i * 4 + 2)
                apart(pe)
                for j in range(TG):
                    last = t_.transpose(ps[3 + j // 4][0:32, (j % 4) * P:(j % 4) * P + P], edgeA[:, j, :], ident[:, :])
                last.then_inc(sgp, 1)
                rowM = rowD[:, :].bitcast(f32)
                pe.wait_ge(sgv, i * 4 + 4)
                apart(pe)
                for j in range(TG):
                    t_.transpose(ps[5][:, j * 32:j * 32 + 32], rowM[:, j * P:(j + 1) * P], ident[0:32, 0:32])
                for j in range(TG):
                    last = t_.transpose(ps[5][:, 256 + j * GS:256 + j * GS + GS],
                                        rowF[0:GS, j * P:(j + 1) * P], ident[0:GS, 0:GS])
                last.then_inc(sgp, 1)

            def sums(k, h):
                k.after(f"sf{h}", 2)
                k.after(f"y{h}", 2)
                bank = pu[:, ds((k.sn % 2) * 512, YW)]
                for t in range(h * 4, h * 4 + 4):
                    last = t_.matmul(bank, Sf[:, t, :], Y[:, t, :], start=(t == 0),
                                     stop=(t == 7))
                last.then_inc(L[1][f"U{h}"], 1)

            def turn(k):
                if k.has(2):
                    k.after("tm", 4)
                    sums(k, 0)
                if k.has(0):
                    transposes(k, (k.sn % 2) * TG)
                if k.has(2):
                    sums(k, 1)
                if k.has(0):
                    dests = adp[:, ds(k.b, 1), :, :].rearrange("p b k h -> p (b k h)")
                    k.after("adx", 1)
                    for h in range(2):
                        k.after(f"sts{h}", 0)
                        for t in range(h * 4, h * 4 + 4):
                            last = t_.matmul(ps[2][:, t * 3 * H:(t + 1) * 3 * H], ST[:, t, :], dests,
                                             start=True, stop=True)
                    last.then_inc(L[1]["ad"], 1)

            first1 = first_block(pe, "pe_first1")

            def steps1(i, q, half):
                turns(i)
                steps(pe, 1, i, first1, turn)

            prime(pe, 1, "stp0 stp1 ad U0 U1")
            pe.wait_ge(clean, 2)
            supers(pe, steps1)
            tails(pe, 1, turn)

            pe.wait_ge(s["wf"], 16 * (H + 1))
            with pe.Fori(0, NB // 2) as k:
                pe.wait_ge(fin["st"], k + 1)
                for j in range(2):
                    for u in range(2):
                        last = t_.transpose(ps[4][:, (j * 2 + u) * P:(j * 2 + u + 1) * P],
                                            Y[:, j, u * P:u * P + P], ident[:, :])
                last.then_inc(fin["tp"], 1)
                pe.wait_ge(fin["tc"], k + 1)
                pe.wait_ge(fin["v"], k + 1)
                for j in range(2):
                    o = ps[6][:, j * D:j * D + D]
                    t_.matmul(o, Sf[:, j * 2, :], wf[:, 0, :], start=True, stop=False)
                    t_.matmul(o, Sf[:, j * 2 + 1, :], wf[:, 1, :], start=False, stop=False)
                    last = t_.matmul(o, ones[:, :], biasr[:, :], start=False, stop=True)
                last.then_inc(fin["m"], 1)

        @block.scalar
        def _(act):
            a_ = nc.scalar
            with nc.allow_non_contiguous_dma(reason="one destination per group"):
                act.dma_start(Bt[0:1, GS:GS + NG], dst.rearrange("(g e) -> g e", e=64)[0::GE // 64, 0:1]
                              .rearrange("g e -> e g")).then_inc(s["b_ld"], 16)
            for k, a in enumerate((src, dst)):
                if k:
                    act.wait_ge(s["rf"], 1)
                act.dma_start(rows_i[:, 0:(NC - 1) * P].rearrange("p (c e) -> p c e", e=P),
                              a[0:(NC - 1) * P * P].rearrange("(c p e) -> p c e", p=P, e=P)
                              ).then_inc(s["rows_in"], 16)
                act.dma_start(rows_i[0:RL, (NC - 1) * P:NC * P],
                              a[(NC - 1) * P * P:E].rearrange("(p e) -> p e", e=P)).then_inc(s["rows_in"], 16)
            for k, table in enumerate((srcT, dstT)):
                for q in range(NU):
                    act.wait_ge(s["rt"], k * NU + q + 1)
                    n = min(4 * P, NT - q * 4 * P)
                    a_.copy(table[:, q * 4 * P:q * 4 * P + n], ps[(k * NU + q) % 2][:, 0:n]).then_inc(s["rc"], 1)

            def copied(m, rows):
                with act.Fori(0, NB // 2) as k:
                    act.wait_ge(m["tp"], k + 1)
                    a_.copy(stT[0:rows, :, :], ps[4][0:rows, 0:2 * P].rearrange("p (a b) -> p a b", a=2)
                            ).then_inc(m["tc"], 1)

            copied(tab0, D + 1)
            act.wait_ge(s["bt"], 2)

            def to_sbuf(k):
                for h in range(2):
                    k.after(f"stp{h}", 0)
                    a_.copy(ST[:, h * 4:h * 4 + 4, :],
                            ps[h][:, 0:2 * P].bitcast(bf16).rearrange("p (t n) -> p t n", t=4)
                            ).then_inc(L[k.l][f"sts{h}"], 1)

            def turn0(k):
                m = L[0]
                if k.has(0):
                    to_sbuf(k)
                if k.has(2):
                    k.after("U", 3)
                    k.after("h2", 2)
                    a_.copy(h2p[:, 0, :], h2).then_inc(m["hi"], 1)
                if k.has(1):
                    for h in range(2):
                        k.after(f"htp{h}", 1)
                        a_.copy(h1T[:, h * 2:h * 2 + 2, :], ps[2 + h][:, 0:2 * P].rearrange("p (t n) -> p t n", t=2)
                                ).then_inc(m[f"hts{h}"], 1)
                if k.has(2):
                    k.after("rest", 2)
                    a_.copy(h2p[:, 1, :], h2).then_inc(m["mid"], 1)
                if k.has(0):
                    for h in range(2):
                        k.after(f"z{h}", 0)
                        a_.mul(az1[:, h * 4:h * 4 + 4, :],
                               ps[4 + h][:, 0:256].rearrange("p (t d) -> p t d", d=D), 0.01
                               ).then_inc(m[f"az{h}"], 1)
                if k.has(1):
                    k.after("z2", 1)
                    a_.mul(az2, ps[7][:, :], 0.01).then_inc(m["az2"], 1)

            first0 = first_block(act, "act_first0")

            def steps0(i, q, half):
                steps(act, 0, i, first0, turn0)

            prime(act, 0, "sts0 sts1 hts0 hts1 az0 az1 az2 hi mid")
            act.wait_ge(clean, 1)
            supers(act, steps0)
            tails(act, 0, turn0)

            def roots(base):
                with act.Fori(0, NCH) as c:
                    act.wait_ge(lna, c * 2 + (base * 2 * NCH + 1))
                    vv = var[:, ds(c * BC, BC)]
                    a_.activation(vv, vv, ACT.Sqrt).then_inc(lna, 1)

            roots(0)
            copied(tab1, D)

            act_tiles = Past(act, "act_tile", 2, 2 * TS - TG)
            act_blocks = Past(act, "act_block", 3, NB - 1)

            def ends(k, h, back):
                k.after(f"U{h}", back + 1)
                at = act_tiles.back(back - max(k.tail, 0))
                a_.copy(Y[:, h * 4:h * 4 + 4, UW:YW], edgeE[:, ds(at + h * 4, 4), :])
                a_.copy(Sf[:, h * 4:h * 4 + 4, :], S[:, ds(((k.sn + back) % 2) * TG + 4 * h, 4), :]
                        ).then_inc(L[1][f"sf{h}"], 1)

            def turn1(half):
                m = L[1]

                def turn(k):
                    if k.has(2):
                        ends(k, 1, 2)
                    if k.has(3):
                        k.after("dd", 3)
                        a_.activation(ee[:, :, :], dd[:, :, :], ACT.Exp).then_inc(m["e"], 1)
                        b = act_blocks.back(3 - max(k.tail, 0))
                        a_.copy(Mx[:, ds(b, 1), :], mnew[:, :].unsqueeze(1)).then_inc(m["mb"], 1)
                    if k.has(3):
                        k.after("e", 3)
                        for h in range(H):
                            a = a_.activation(Tm[:, h, :], pu[:, ds(((k.sn + 1) % 2) * 512 + h * (D + 1), D + 1)],
                                              ACT.Copy, scale=ee[:, 1, h:h + 1])
                        a.then_inc(m["tm"], 1)
                    if k.has(1):
                        ends(k, 0, 1)
                    if k.has(0):
                        to_sbuf(k)
                    if k.has(1):
                        k.after("y1", 2)
                        a_.activation(wb[:, :, :], dw[:, :, :], ACT.Exp).then_inc(m["w"], 1)
                    if k.has(0):
                        act_tiles.push(k.r * TG + half * TS)
                        act_blocks.push(k.b)
                return turn

            first1 = first_block(act, "act_first1")

            def steps1(i, q, half):
                a_.activation(warm[:, 1:2], warm[:, 0:1], ACT.Exp)
                steps(act, 1, i, first1, turn1(half))

            prime(act, 1, "sts0 sts1 w sf0 sf1 e mb tm")
            act.wait_ge(clean, 2)
            act.wait_ge(sgv, 5)
            supers(act, steps1)
            tails(act, 1, turn1(0))

            with act.Fori(0, NB // 2) as k:
                act.wait_ge(fin["tp"], k + 1)
                a_.copy(Sf[:, 0:4, :], ps[4][:, :].rearrange("p (t n) -> p t n", t=4)).then_inc(fin["tc"], 1)
            roots(1)


_IN = ["x", "src", "dst", "L0_gnn_W1", "L0_gnn_b1", "L0_gnn_W2", "L0_gnn_b2", "L1_gnn_W", "L1_gnn_att_src",
       "L1_gnn_att_dst", "L1_gnn_bias"]


def kernel(**inputs):
    import numpy as _np
    import concourse.bacc as _bacc
    from concourse import mybir as _mybir
    from concourse.bass_utils import run_bass_kernel_spmd as _run

    nc = _bacc.Bacc("TRN2", target_bir_lowering=False, num_devices=1)
    f32, i32 = _mybir.dt.float32, _mybir.dt.int32
    arrays, args = {}, []
    for name in _IN:
        a = _np.ascontiguousarray(inputs[name])
        arrays["in_" + name] = a
        args.append(nc.dram_tensor("in_" + name, a.shape, _mybir.dt.from_np(a.dtype), kind="ExternalInput").ap())
    args.append(nc.dram_tensor("out_0", (N, D), f32, kind="ExternalOutput").ap())
    for name, shape, dt in (("q_dram", (NB * P, BF), _mybir.dt.bfloat16), ("x_dram", (NB * P, XW), f32),
                            ("srcT_dram", (P, T), i32), ("dstT_dram", (P, T), f32), ("dst_dram", (EP,), i32)):
        args.append(nc.dram_tensor(name, shape, dt, kind="Internal").ap())
    build(nc, *args)
    r = _run(nc, [arrays], core_ids=[0])
    return r.results[0]["out_0"]
```
